# Optimizing a Trainium2 kernel written in Bass

```python
import numpy as np
import jax
import jax.numpy as jnp

def _softmax(x, axis=-1):
    return jax.nn.softmax(x, axis=axis)

def _gelu(x):
    return jax.nn.gelu(x, approximate=True)

def _silu(x):
    return jax.nn.silu(x)

def _sigmoid(x):
    return jax.nn.sigmoid(x)

def _layernorm(x, axis=-1, eps=1e-05):
    m = jnp.mean(x, axis=axis, keepdims=True)
    v = jnp.var(x, axis=axis, keepdims=True)
    return (x - m) / jnp.sqrt(v + eps)

def _scatter_add(tgt, idx, src, axis=0):
    return tgt.at[idx].add(src)

def _segment_sum(src, seg, n):
    return jax.ops.segment_sum(src, seg, n)
kernel_name = 'mk_decoder_preln_d1_seqx_r8_18fdbc'

def setup_inputs(seed: int=0):
    np.random.seed(seed)
    _w = jnp.asarray

    def _rec_inputs():
        import jax
        import jax.numpy as jnp
        _rk = jax.random.key(seed)
        x = 7.22e-05 + 1 * jax.random.normal(jax.random.fold_in(_rk, 1), (64, 64, 256), jnp.float32)
        _lenS = 64 - jax.random.randint(jax.random.fold_in(_rk, 7), (64,), 0, max(1, 64 // 4) + 1, jnp.int32)
        _lenS2 = 64 - jax.random.randint(jax.random.fold_in(_rk, 8), (64,), 0, max(1, 64 // 4) + 1, jnp.int32)
        _ctx_512P = jax.random.normal(jax.random.fold_in(_rk, 11), (64, 16, 64), jnp.float32)
        _ctx_512c = jax.random.dirichlet(jax.random.fold_in(_rk, 511), 0.3 * jnp.ones((16,), jnp.float32), (64, 64))
        _ctx_512t = jnp.einsum('bsk,bkd->bsd', _ctx_512c, _ctx_512P)
        _ctx_512t = _ctx_512t * jax.lax.rsqrt(jnp.mean(jnp.square(_ctx_512t)) + 1e-12) * 0.953939
        ctx_512 = -0.000514642 + 1.00011 * (_ctx_512t + 0.3 * jax.random.normal(jax.random.fold_in(_rk, 611), (64, 64, 64), jnp.float32))
        return (x, ctx_512)
    x, ctx_512 = _rec_inputs()

    def _L0_attn_setup():
        import jax, jax.numpy as jnp
        import numpy as np
        H = 256
        HK = 16
        HV = 32
        DK = 128
        DV = 128
        KC = 4
        VE = HV // HK * DV
        B, T = (1, 64)

        def _causal_conv_silu(x, w, b):
            t = x.shape[1]
            kk = w.shape[1]
            xp = jnp.pad(x, ((0, 0), (kk - 1, 0), (0, 0)))
            y = b
            for j in range(kk):
                y = y + w[:, j] * xp[:, j:j + t, :]
            return jax.nn.silu(y)

        def _l2norm(x):
            return x / jnp.maximum(jnp.linalg.norm(x, axis=-1, keepdims=True), 1e-12)

        def _reference_tuple_inner(x, Wq, Wk, Wv, Wo, Wa, Wb, qcw, qcb, kcw, kcb, vcw, vcb):
            b, t, _ = x.shape
            q = _causal_conv_silu(x @ Wq, qcw, qcb).reshape(b, t, HK, DK)
            k = _causal_conv_silu(x @ Wk, kcw, kcb).reshape(b, t, HK, DK)
            v = _causal_conv_silu(x @ Wv, vcw, vcb).reshape(b, t, HK, VE)
            q = _l2norm(q)
            k = _l2norm(k)
            alpha = jax.nn.sigmoid(x @ Wa)
            beta = jax.nn.sigmoid(x @ Wb)
            state0 = jnp.zeros((b, HK, DK, VE), x.dtype)

            def step(state, inp):
                qt, kt, vt, at, bt = inp
                state = state * at[:, :, None, None]
                err = vt - jnp.einsum('bhkv,bhk->bhv', state, kt)
                state = state + bt[:, :, None, None] * jnp.einsum('bhk,bhv->bhkv', kt, err)
                ot = jnp.einsum('bhkv,bhk->bhv', state, qt)
                return (state, ot)
            xs = (q.transpose(1, 0, 2, 3), k.transpose(1, 0, 2, 3), v.transpose(1, 0, 2, 3), alpha.transpose(1, 0, 2), beta.transpose(1, 0, 2))
            state, outs = jax.lax.scan(step, state0, xs)
            out = outs.transpose(1, 0, 2, 3).reshape(b, t, HV * DV) @ Wo
            return (out, state)
        key = jax.random.key(seed)
        ks = jax.random.split(key, 13)
        s = 0.02

        def p(k, shape):
            return jax.random.normal(k, shape, jnp.float32) * s
        return {'x': jax.random.normal(ks[0], (B, T, H), jnp.float32), 'Wq': p(ks[1], (H, HK * DK)), 'Wk': p(ks[2], (H, HK * DK)), 'Wv': p(ks[3], (H, HV * DV)), 'Wo': p(ks[4], (HV * DV, H)), 'Wa': p(ks[5], (H, HK)), 'Wb': p(ks[6], (H, HK)), 'qcw': p(ks[7], (HK * DK, KC)), 'qcb': p(ks[8], (HK * DK,)), 'kcw': p(ks[9], (HK * DK, KC)), 'kcb': p(ks[10], (HK * DK,)), 'vcw': p(ks[11], (HV * DV, KC)), 'vcb': p(ks[12], (HV * DV,))}
    _L0_attn_all = _L0_attn_setup()
    _L0_attn_in = {k: v for k, v in _L0_attn_all.items() if k in ('Wq', 'Wk', 'Wv', 'Wo', 'Wa', 'Wb', 'qcw', 'qcb', 'kcw', 'kcb', 'vcw', 'vcb')}
    del _L0_attn_all

    def _L0_xattn_setup():
        import jax, jax.numpy as jnp
        import numpy as np
        B, S, E = (2, 256, 256)
        QH, KVH = (32, 8)
        D = E // QH
        G = QH // KVH
        DROPOUT = 1.0
        key = jax.random.key(seed)
        k1, k2, k3 = jax.random.split(key, 3)
        q = jax.random.normal(k1, (B, S, E), dtype=jnp.float32)
        k = jax.random.normal(k2, (B, S, E // G), dtype=jnp.float32)
        v = jax.random.normal(k3, (B, S, E // G), dtype=jnp.float32)
        return {'q': q, 'k': k, 'v': v}
    _L0_xattn_all = _L0_xattn_setup()
    _L0_xattn_in = {k: v for k, v in _L0_xattn_all.items() if k in ()}
    del _L0_xattn_all

    def _L0_ffn_setup():
        import jax, jax.numpy as jnp
        import numpy as np
        EPS = 1e-08

        def _bit_quant(w):
            scale = jnp.maximum(jnp.mean(jnp.abs(w)), EPS)
            w_ternary = jnp.clip(jnp.round(w / scale), -1.0, 1.0)
            return w + jax.lax.stop_gradient(w_ternary - w)
        key = jax.random.key(seed)
        k = jax.random.split(key, 5)
        emb, dff = (256, 1024)
        B, S = (4, 256)
        x = jax.random.normal(k[0], (B, S, emb), dtype=jnp.float32)
        w1 = jax.random.normal(k[1], (dff, emb), dtype=jnp.float32) * 0.02
        b1 = jax.random.normal(k[2], (dff,), dtype=jnp.float32) * 0.02
        w2 = jax.random.normal(k[3], (emb, dff), dtype=jnp.float32) * 0.02
        b2 = jax.random.normal(k[4], (emb,), dtype=jnp.float32) * 0.02
        return {'x': x, 'w1': w1, 'b1': b1, 'w2': w2, 'b2': b2}
    _L0_ffn_all = _L0_ffn_setup()
    _L0_ffn_in = {k: v for k, v in _L0_ffn_all.items() if k in ('w1', 'b1', 'w2', 'b2')}
    del _L0_ffn_all
    return {'x': x, 'ctx_512': ctx_512, 'L0_attn_Wq': _L0_attn_in['Wq'], 'L0_attn_Wk': _L0_attn_in['Wk'], 'L0_attn_Wv': _L0_attn_in['Wv'], 'L0_attn_Wo': _L0_attn_in['Wo'], 'L0_attn_Wa': _L0_attn_in['Wa'], 'L0_attn_Wb': _L0_attn_in['Wb'], 'L0_attn_qcw': _L0_attn_in['qcw'], 'L0_attn_qcb': _L0_attn_in['qcb'], 'L0_attn_kcw': _L0_attn_in['kcw'], 'L0_attn_kcb': _L0_attn_in['kcb'], 'L0_attn_vcw': _L0_attn_in['vcw'], 'L0_attn_vcb': _L0_attn_in['vcb'], 'L0_ffn_w1': _L0_ffn_in['w1'], 'L0_ffn_b1': _L0_ffn_in['b1'], 'L0_ffn_w2': _L0_ffn_in['w2'], 'L0_ffn_b2': _L0_ffn_in['b2']}

def reference(x, ctx_512, L0_attn_Wq, L0_attn_Wk, L0_attn_Wv, L0_attn_Wo, L0_attn_Wa, L0_attn_Wb, L0_attn_qcw, L0_attn_qcb, L0_attn_kcw, L0_attn_kcb, L0_attn_vcw, L0_attn_vcb, L0_ffn_w1, L0_ffn_b1, L0_ffn_w2, L0_ffn_b2):
    import jax
    import jax.numpy as jnp

    def _L0_attn_ref(x, Wq, Wk, Wv, Wo, Wa, Wb, qcw, qcb, kcw, kcb, vcw, vcb):
        import jax, jax.numpy as jnp
        import numpy as np
        H = 256
        HK = 16
        HV = 32
        DK = 128
        DV = 128
        KC = 4
        VE = HV // HK * DV
        B, T = (1, 64)

        def _causal_conv_silu(x, w, b):
            t = x.shape[1]
            kk = w.shape[1]
            xp = jnp.pad(x, ((0, 0), (kk - 1, 0), (0, 0)))
            y = b
            for j in range(kk):
                y = y + w[:, j] * xp[:, j:j + t, :]
            return jax.nn.silu(y)

        def _l2norm(x):
            return x / jnp.maximum(jnp.linalg.norm(x, axis=-1, keepdims=True), 1e-12)

        def _reference_tuple_inner(x, Wq, Wk, Wv, Wo, Wa, Wb, qcw, qcb, kcw, kcb, vcw, vcb):
            b, t, _ = x.shape
            q = _causal_conv_silu(x @ Wq, qcw, qcb).reshape(b, t, HK, DK)
            k = _causal_conv_silu(x @ Wk, kcw, kcb).reshape(b, t, HK, DK)
            v = _causal_conv_silu(x @ Wv, vcw, vcb).reshape(b, t, HK, VE)
            q = _l2norm(q)
            k = _l2norm(k)
            alpha = jax.nn.sigmoid(x @ Wa)
            beta = jax.nn.sigmoid(x @ Wb)
            state0 = jnp.zeros((b, HK, DK, VE), x.dtype)

            def step(state, inp):
                qt, kt, vt, at, bt = inp
                state = state * at[:, :, None, None]
                err = vt - jnp.einsum('bhkv,bhk->bhv', state, kt)
                state = state + bt[:, :, None, None] * jnp.einsum('bhk,bhv->bhkv', kt, err)
                ot = jnp.einsum('bhkv,bhk->bhv', state, qt)
                return (state, ot)
            xs = (q.transpose(1, 0, 2, 3), k.transpose(1, 0, 2, 3), v.transpose(1, 0, 2, 3), alpha.transpose(1, 0, 2), beta.transpose(1, 0, 2))
            state, outs = jax.lax.scan(step, state0, xs)
            out = outs.transpose(1, 0, 2, 3).reshape(b, t, HV * DV) @ Wo
            return (out, state)
        return _reference_tuple_inner(x, Wq, Wk, Wv, Wo, Wa, Wb, qcw, qcb, kcw, kcb, vcw, vcb)[0]

    def _L0_xattn_ref(q, k, v):
        import jax, jax.numpy as jnp
        import numpy as np
        B, S, E = (2, 256, 256)
        QH, KVH = (32, 8)
        D = E // QH
        G = QH // KVH
        DROPOUT = 1.0
        b, s, _ = q.shape
        qh = q.reshape(b, s, KVH, G, D).transpose(0, 2, 3, 1, 4)
        kh = k.reshape(b, s, KVH, D).transpose(0, 2, 1, 3)
        vh = v.reshape(b, s, KVH, D).transpose(0, 2, 1, 3)
        scale = 1.0 / jnp.sqrt(jnp.float32(D))
        scores = jnp.einsum('bkgsd,bktd->bkgst', qh, kh) * scale
        attn = jax.nn.softmax(scores, axis=-1) / DROPOUT
        out = jnp.einsum('bkgst,bktd->bkgsd', attn, vh)
        return out.transpose(0, 3, 1, 2, 4).reshape(b, s, E)

    def _L0_ffn_ref(x, w1, b1, w2, b2):
        import jax, jax.numpy as jnp
        import numpy as np
        EPS = 1e-08

        def _bit_quant(w):
            scale = jnp.maximum(jnp.mean(jnp.abs(w)), EPS)
            w_ternary = jnp.clip(jnp.round(w / scale), -1.0, 1.0)
            return w + jax.lax.stop_gradient(w_ternary - w)
        w1q = _bit_quant(w1)
        w2q = _bit_quant(w2)
        h = jnp.einsum('bsd,fd->bsf', x, w1q) + b1
        h = jax.nn.gelu(h, approximate=False)
        return jnp.einsum('bsf,df->bsd', h, w2q) + b2
    x = x + _L0_attn_ref(_layernorm(x, axis=-1), L0_attn_Wq, L0_attn_Wk, L0_attn_Wv, L0_attn_Wo, L0_attn_Wa, L0_attn_Wb, L0_attn_qcw, L0_attn_qcb, L0_attn_kcw, L0_attn_kcb, L0_attn_vcw, L0_attn_vcb)
    x = x + _L0_xattn_ref(_layernorm(x, axis=-1), ctx_512, ctx_512)
    x = x + _L0_ffn_ref(_layernorm(x, axis=-1), L0_ffn_w1, L0_ffn_b1, L0_ffn_w2, L0_ffn_b2)
    return x

_drawn_inputs = setup_inputs


def setup_inputs(seed=0):
    import zlib

    import numpy as np

    out = dict(_drawn_inputs(seed))
    spreads = {}
    factors = {'L0_attn_Wq': 8.0,
     'L0_attn_Wk': 8.0,
     'L0_attn_Wv': 8.0,
     'L0_attn_Wo': 8.0,
     'L0_attn_Wa': 8.0,
     'L0_attn_Wb': 8.0,
     'L0_attn_qcw': 8.0,
     'L0_attn_qcb': 8.0,
     'L0_attn_kcw': 8.0,
     'L0_attn_kcb': 8.0,
     'L0_attn_vcw': 8.0,
     'L0_attn_vcb': 8.0,
     'L0_ffn_b1': 38.045,
     'L0_ffn_b2': 64.0}
    for name, (base, spread) in spreads.items():
        noise = np.random.default_rng([zlib.crc32(name.encode()), seed]).standard_normal(out[name].shape)
        drawn = base * np.exp(spread * noise) if base else spread * noise
        out[name] = jnp.asarray(drawn.astype(out[name].dtype))
    for name, factor in factors.items():
        out[name] = (out[name] * factor).astype(out[name].dtype)
    return out
```

```python
from contextlib import ExitStack

import numpy as np
import concourse.bass as bass
from concourse import mybir

ALU = mybir.AluOpType
ACT = mybir.ActivationFunctionType
F32 = mybir.dt.float32
F16 = mybir.dt.float16
AX_X = mybir.AxisListType.X
ds = bass.ds

P = 128
T = 64
E = 256
NB = 64
GT = 512
G = NB * T // GT
NP = GT // P
NH = 16
DK = 128
LV = 6
CD = 64
F = 1024
FB = F // P
WS = 64.0
D8 = 8

C_ID, C_IC, C_MT = 0, 128, 192
C_UT, C_LE, C_ON = C_MT + 64 * LV, C_MT + 64 * LV + 128, C_MT + 64 * LV + 256
C_UTC = C_ON + 128
C_LEC, C_MA, C_MQ = C_UTC + 64, C_UTC + 128, C_UTC + 192
C_REP = C_MQ + 64
C_GM = C_REP + 256
NCST = C_GM + 4


def constants():
    c = np.zeros((P, NCST), np.float32)
    p = np.arange(P)[:, None]
    q = np.arange(P)[None, :]
    s, j = p % T, np.arange(T)[None, :]
    same = (p // T) == (q // T)
    c[:, C_ID:C_ID + 128] = p == q
    c[:, C_IC:C_IC + 64] = s == j
    for k in range(LV):
        c[:, C_MT + 64 * k:C_MT + 64 * k + 64] = ((s >> (k + 1)) == (j >> (k + 1))) & ((s >> k) % 2 == 0) & ((j >> k) % 2 == 1)
    c[:, C_UT:C_UT + 128] = same & (p < q)
    c[:, C_LE:C_LE + 128] = same & (p >= q)
    c[:, C_ON:C_ON + 128] = same
    c[:, C_UTC:C_UTC + 64] = s < j
    c[:, C_LEC:C_LEC + 64] = s >= j
    c[:, C_MA:C_MA + 64] = s > j
    c[:, C_MQ:C_MQ + 64] = s <= j
    for half in range(2):
        for m in range(P):
            c[(half * 4 + m // 32) * D8 + m % D8, C_REP + 128 * half + m] = 1.0
    c[:, C_GM:C_GM + 4] = (p // D8) % 4 == np.arange(4)[None, :]
    return c


def build(nc, x, ctxT, ctxR, wall, wo, wab, cw, w1, b1, w2, b2, cst, out):
    ctx = ExitStack()
    with ctx:
        def sb(name, shape, dt=F32):
            return ctx.enter_context(nc.sbuf_tensor(name, shape, dt))

        def sem(name):
            return ctx.enter_context(nc.semaphore(name))

        WH = sb("WH", [P, 2, NH * 512], F16)
        WL = sb("WL", [P, 2, NH * 512], F16)
        WO = sb("WO", [P, 2 * NH, E])
        SCR = sb("SCR", [P, 8192])
        CST = sb("CST", [P, NCST])
        CW = sb("CW", [P, NH, 20])
        CWC = sb("CWC", [P, 20])
        AB32 = sb("AB32", [P, 2, 32])
        ABH = sb("ABH", [P, 2, 32], F16)
        ABL = sb("ABL", [P, 2, 32], F16)
        W1 = sb("W1", [P, 2, F], F16)
        W2 = sb("W2", [P, FB, E], F16)
        B1 = sb("B1", [P, FB])
        B2 = sb("B2", [P, E])
        XP = sb("XP", [P, NP, E])
        XC = sb("XC", [P, NP, E])
        XH = sb("XH", [P, 2, GT + 1], F16)
        XL = sb("XL", [P, 2, GT + 1], F16)
        STT6 = sb("STT6", [P, NP, 6])
        MV = sb("MV", [P, NP, 2])
        RSTD = sb("RSTD", [P, NP])
        VE = sb("VE", [P, NP])
        SSM = sb("SSM", [P, 2 * NP])
        MHALF = sb("MHALF", [P, 2 * NP])
        ZS = sb("ZS", [P, NP, 32])
        LA = sb("LA", [P, NP, NH])
        LT = sb("LT", [P, 4, NP, NH])
        BE = sb("BE", [P, NH, NP])
        KQ = sb("KQ", [P, 2, GT])
        Y = sb("Y", [P, 4, GT])
        V = sb("V", [P, NP, 256])
        SQ = sb("SQ", [P, 2, GT])
        XN = SQ[:, :, :].rearrange("p a (b e) -> p (a b) e", e=E)
        NQ = sb("NQ", [P, 2, NP])
        NBT = sb("NBT", [P, NP])
        RA = sb("RA", [P, NP])
        EAM = sb("EAM", [P, NP, T])
        EQM = sb("EQM", [P, NP, T])
        EAR = sb("EAR", [P, NP, T])
        A = sb("A", [P, NP, P])
        X = sb("X", [P, NP, P])
        M = sb("M", [P, NP, P])
        GQ = sb("GQ", [P, NP, T])
        W = sb("W", [P, NP, T])
        Z = sb("Z", [P, NP, T])
        T1 = sb("T1", [P, NP, T])
        DQ = sb("DQ", [P, NP, T])
        OT = sb("OT", [P, 2, GT])
        CT = sb("CT", [CD, GT])
        VT = sb("VT", [P, 8, CD])
        VB = sb("VB", [P, 64, 2, 9])
        MX = sb("MX", [P, 4, 8])
        RS = sb("RS", [P, 32])
        OB = sb("OB", [P, 32, D8])
        SMALL = sb("SMALL", [P, 8])
        ONES = sb("ONES", [P, 1])
        ZW = sb("ZW", [P, P], F16)

        EA = SCR[:, 0:4096].rearrange("p (h a t) -> p h a t", h=NH, a=NP)
        EQ = SCR[:, 4096:8192].rearrange("p (h a t) -> p h a t", h=NH, a=NP)
        KG = SCR[:, 0:4096].rearrange("p (c b g t) -> p c b g t", c=2, b=8, g=4)
        ES = SCR[:, 4096:6144].rearrange("p (c r g t) -> p c r g t", c=2, r=4, g=4)
        PT = SCR[:, 6144:8192].rearrange("p (r q s) -> p r q s", r=4, q=4)
        H = SCR[:, 0:4096].rearrange("p (f t) -> p f t", f=FB)
        HH = SCR[:, 4096:6144].bitcast(F16).rearrange("p (f t) -> p f t", f=FB)
        HL = SCR[:, 6144:8192].bitcast(F16).rearrange("p (f t) -> p f t", f=FB)
        QT = KQ
        RHA = Y[:, 0:2, :].rearrange("p a (b t) -> p (a b) t", t=T)
        RHQ = Y[:, 2:4, :].rearrange("p a (b t) -> p (a b) t", t=T)

        ident = CST[:, C_ID:C_ID + 128]
        identc = CST[:, C_IC:C_IC + 64]

        def mt(k):
            return CST[:, C_MT + 64 * k:C_MT + 64 * k + 64]

        def over_pairs(m, n=NP):
            return m[:, None, :].broadcast_to([P, n, T])

        PJ = [ctx.enter_context(nc.psum_tensor(f"PJ{i}", [P, GT], F32)) for i in range(2)]
        GR, CH, BD, SP = [ctx.enter_context(nc.psum_tensor(n, [P, GT], F32)) for n in ("GR", "CH", "BD", "SP")]
        AC = [ctx.enter_context(nc.psum_tensor(f"AC{i}", [P, GT], F32)) for i in range(2)]
        gram = GR[:, :].rearrange("p (a k t) -> p a k t", a=NP, k=2)
        psW = CH[:, 0:256].rearrange("p (a t) -> p a t", a=NP)
        psP = CH[:, 256:512].rearrange("p (a t) -> p a t", a=NP)
        psR = BD[:, 0:256].rearrange("p (a t) -> p a t", a=NP)
        psX = BD[:, :].rearrange("p (a t) -> p a t", a=NP)

        names = """ld_const ld_w0 ld_w1 ld_w2 ld_w3
            w_split w_hi tern_sum tern_all tern_done zeroed conv_scaled""".split()
        owned = {
            "sync": "ld_x ld_ctx st_out",
            "pool": "x_copied rhq_done masked rsq sq rstd vb_done",
            "act": "xh_done gate_s dec_exp tap kq x_bd ot_done v_done exp_done pt_done gelu_done",
            "dve": """ln_step xl_done gate_v rha_done cw_cur conv scale_done dq_done a_done gq_done t1_done w_done_v z_done m_done
                      x1_done kg_done mx_done sub_done rs_done ob_done nrm_done hh_done hl_done y_done x3_done""",
            "pe": """tr_done gate_mm dec_mm proj gram_mm ss_mm r_mm w_mm t_mm p_mm m_mm o_mm vt_mm op_mm
                     rep_mm sc_mm pt_mm pv_mm f1_mm f2_mm""",
        }
        names += " ".join(owned.values()).split()
        S = {n: sem(n) for n in names}
        LW = [S[f"ld_w{n}"] for n in range(4)]

        def start_counts(eng, who):
            for n in owned[who].split():
                eng.sem_inc(S[n], 1)

        def at(count):
            return count + 1

        block = ctx.enter_context(nc.Block())

        @block.sync
        def _(sp):
            start_counts(sp, "sync")
            sp.dma_start(CST[:, :], cst).then_inc(S["ld_const"], 16)
            sp.dma_start(CW[:, :, :], cw).then_inc(S["ld_const"], 16)
            sp.dma_start(AB32[:, :, :], wab).then_inc(S["ld_const"], 16)
            sp.dma_start(B1[:, :], b1).then_inc(S["ld_const"], 16)
            sp.dma_start(B2[:, :], b2).then_inc(S["ld_const"], 16)
            sp.dma_start(XP[:, :, :], x[0]).then_inc(S["ld_x"], 16)
            for n in range(8):
                if n >= 4:
                    sp.wait_ge(S["w_split"], n - 3)
                sp.dma_start(SCR[:, (n % 4) * 2048:(n % 4 + 1) * 2048],
                             wall[n // 4][:, (n % 4) * 2048:(n % 4 + 1) * 2048]).then_inc(LW[n % 4], 16)
            sp.dma_start(WO[:, :, :], wo).then_inc(S["ld_const"], 16)
            sp.wait_ge(S["w_split"], 6)
            sp.dma_start(SCR[:, 0:2048], w1).then_inc(LW[0], 16)
            sp.dma_start(SCR[:, 2048:4096], w2).then_inc(LW[1], 16)

            def group(g, last):
                sp.wait_ge(S["kg_done"], at(g * 2))
                sp.wait_ge(S["vb_done"], at(g * 2))
                one = ds(g, 1)
                sp.dma_start(CT[:, :], ctxT[one].rearrange("a c t -> (a c) t")).then_inc(S["ld_ctx"], 16)
                sp.dma_start(VT[0:64, :, :], ctxR[one].rearrange("a t b c -> (a t) b c")).then_inc(S["ld_ctx"], 16)
                sp.dma_start(VT[64:128, :, :], ctxR[one].rearrange("a t b c -> (a t) b c")).then_inc(S["ld_ctx"], 16)
                if not last:
                    sp.wait_ge(S["x_copied"], at(g + 1))
                    sp.wait_ge(S["ln_step"], at(g * 39 + 13))
                    sp.dma_start(XP[:, :, :], x[ds(g + 1, 1)].rearrange("a p n e -> (a p) n e")).then_inc(S["ld_x"], 16)
                sp.wait_ge(S["x3_done"], at(g * 2 + 2))
                sp.dma_start(out[one].rearrange("a p n e -> (a p) n e"), XC[:, :, :]).then_inc(S["st_out"], 16)

            with sp.Fori(0, G - 1) as g:
                group(g, False)
            group(G - 1, True)
            sp.wait_ge(S["st_out"], at(16 * G))

        @block.gpsimd
        def _(pool):
            start_counts(pool, "pool")
            pool.wait_ge(S["tern_sum"], 2)
            nc.gpsimd.partition_all_reduce(SMALL[:, 2:4], SMALL[:, 0:2], P, bass.bass_isa.ReduceOp.add).then_inc(S["tern_all"], 1)
            nc.gpsimd.memset(VB[:, :, :, :], 0.0).then_inc(S["zeroed"], 1)
            pool.wait_ge(S["zeroed"], 1)
            nc.gpsimd.memset(VB[:, :, :, 8:9], 0.0).then_inc(S["zeroed"], 1)
            pool.wait_ge(S["zeroed"], 2)
            nc.gpsimd.memset(VB[0:64, :, 0, 8:9], 1.0).then_inc(S["zeroed"], 1)
            pool.wait_ge(S["zeroed"], 3)
            nc.gpsimd.memset(VB[64:128, :, 1, 8:9], 1.0).then_inc(S["zeroed"], 1)
            pool.wait_ge(S["zeroed"], 4)
            nc.gpsimd.memset(MHALF[:, :], -0.5).then_inc(S["zeroed"], 1)
            pool.wait_ge(S["zeroed"], 5)
            pool.wait_ge(S["ld_const"], 96)

            def rstd(nid):
                pool.wait_ge(S["ln_step"], at(nid * 13 + 9))
                nc.gpsimd.tensor_tensor(RSTD[:, :], VE[:, :], MHALF[:, 0:NP], ALU.pow).then_inc(S["rstd"], 1)

            def inverse_norms(it):
                pool.wait_ge(S["scale_done"], at(it * 4 + 1))
                nc.gpsimd.tensor_tensor(NQ[:, :, :].rearrange("p k a -> p (k a)"), SSM[:, :], MHALF[:, :], ALU.pow).then_inc(S["rsq"], 1)

            def masked(it, h):
                pool.wait_ge(S["scale_done"], at(it * 4))
                nc.gpsimd.tensor_tensor(EAM[:, :, :], EA[:, ds(h, 1), :, :].rearrange("p o a t -> p (o a) t"),
                                        over_pairs(CST[:, C_MA:C_MA + 64]), ALU.mult).then_inc(S["masked"], 1)
                pool.wait_ge(S["gq_done"], at(it))
                nc.gpsimd.tensor_tensor(EQM[:, :, :], EQ[:, ds(h, 1), :, :].rearrange("p o a t -> p (o a) t"),
                                        over_pairs(CST[:, C_MQ:C_MQ + 64]), ALU.mult).then_inc(S["masked"], 1)

            def squares(it):
                pool.wait_ge(S["ss_mm"], at(it))
                for n, a in enumerate((1, 0)):
                    pool.wait_ge(S["kq"], at(it * 2 + n + 1))
                    nc.gpsimd.tensor_tensor(SQ[:, a, :], KQ[:, a, :], KQ[:, a, :], ALU.mult).then_inc(S["sq"], 1)

            with pool.Fori(0, G) as g:
                pool.wait_ge(S["ld_x"], at(g * 16 + 16))
                pool.wait_ge(S["st_out"], at(g * 16))
                pool.nop(nofuse=True)
                nc.gpsimd.tensor_copy(XC[:, :, :], XP[:, :, :]).then_inc(S["x_copied"], 1)
                rstd(g * 3)
                pool.wait_ge(S["gate_v"], at(g * 6 + 6))
                for p in range(NP):
                    if p:
                        pool.wait_ge(S["dec_mm"], at(g * 16 + 4 * p))
                    nc.gpsimd.tensor_tensor(RHQ, CST[:, C_UTC:C_UTC + 64][:, None, :].broadcast_to([P, NH, T]),
                                            LA[:, p, :][:, :, None].broadcast_to([P, NH, T]), ALU.mult).then_inc(S["rhq_done"], 1)
                pool.wait_ge(S["dec_exp"], at(g * 16 + 16))
                squares(g * NH)
                with pool.Fori(1, NH) as h:
                    masked(g * NH + h - 1, h - 1)
                    inverse_norms(g * NH + h - 1)
                    squares(g * NH + h)
                masked(g * NH + NH - 1, NH - 1)
                inverse_norms(g * NH + NH - 1)
                rstd(g * 3 + 1)
                pool.wait_ge(S["ld_ctx"], at(g * 48 + 48))
                pool.wait_ge(S["pv_mm"], at(g * 4))
                pool.nop(nofuse=True)
                for n in range(2):
                    pool.wait_ge(S["vb_done"], at(g * 2 + n))
                    pool.nop(nofuse=True)
                    nc.gpsimd.tensor_copy(VB[64 * n:64 * n + 64, :, n, 0:8],
                                          VT[64 * n:64 * n + 64, :, :].rearrange("p b (k d) -> p (b k) d", d=D8)).then_inc(S["vb_done"], 1)
                pool.wait_ge(S["vb_done"], at(g * 2 + 2))
                rstd(g * 3 + 2)

        @block.scalar
        def _(act):
            start_counts(act, "act")
            for n in range(8):
                act.wait_ge(LW[n % 4], 16 * (n // 4 + 1))
                nc.scalar.activation(WH[:, n // 4, (n % 4) * 2048:(n % 4 + 1) * 2048], SCR[:, (n % 4) * 2048:(n % 4 + 1) * 2048],
                                     ACT.Copy, scale=WS).then_inc(S["w_hi"], 1)

            def transposed(nid, n):
                for c in range(2):
                    act.wait_ge(S["tr_done"], at(nid * 2 + c + 1))
                    if n == 1:
                        nc.scalar.activation(QT[:, c, :], PJ[c][:, :], ACT.Copy).then_inc(S["xh_done"], 1)
                    else:
                        nc.scalar.activation(XH[:, c, 0:GT], PJ[c][:, :], ACT.Copy).then_inc(S["xh_done"], 1)

            def tap(it, b):
                act.wait_ge(S["proj"], at(it * 4 + b + 1))
                act.wait_ge(S["cw_cur"], at(it + 1))
                act.wait_ge(S["vt_mm"], at(it * 2))
                act.wait_ge(S["kq"], at(it * 2))
                nc.scalar.activation(Y[:, b, :], PJ[b % 2][:, :], ACT.Identity, scale=CWC[:, 5 * b + 3:5 * b + 4],
                                     bias=CWC[:, 5 * b + 4:5 * b + 5]).then_inc(S["tap"], 1)

            def silu_kq(it, b):
                act.wait_ge(S["conv"], at(it * 12 + 3 * b + 3))
                act.wait_ge(S["gram_mm"], at(it))
                act.wait_ge(S["sq"], at(it * 2))
                nc.scalar.activation(KQ[:, 1 - b, :], Y[:, b, :], ACT.Silu).then_inc(S["kq"], 1)

            def silu_v(it, b):
                act.wait_ge(S["vt_mm"], at(it * 2 + b - 1))
                act.wait_ge(S["o_mm"], at(it * 2))
                src = (SP, CH)[b - 2]
                nc.scalar.activation(V[:, :, (b - 2) * P:(b - 1) * P], src[:, :].rearrange("p (a n) -> p a n", a=NP),
                                     ACT.Silu).then_inc(S["v_done"], 1)

            def x_diag(it, k):
                act.wait_ge(S["t_mm"], at(it * LV + k))
                if k == 1:
                    act.wait_ge(S["m_mm"], at(it))
                else:
                    act.wait_ge(S["p_mm"], at(it * 5 + k - 1))
                for n in range(2):
                    lo = 64 * n
                    nc.scalar.activation(X[lo:lo + 64, :, lo:lo + 64], psX[0:64, :, lo:lo + 64], ACT.Copy).then_inc(S["x_bd"], 1)

            def o_out(it):
                for n, src in enumerate((GR, BD)):
                    act.wait_ge(S["o_mm"], at(it * 2 + n + 1))
                    act.wait_ge(S["op_mm"], at(it))
                    nc.scalar.activation(OT[:, n, :], src[:, :], ACT.Copy).then_inc(S["ot_done"], 1)

            act.wait_ge(S["ld_const"], 96)
            with act.Fori(0, G) as g:
                transposed(g * 3, 0)
                act.wait_ge(S["gate_v"], at(g * 6 + 3))
                nc.scalar.activation(LT[:, 2], LT[:, 0], ACT.Exp, scale=-1.0).then_inc(S["gate_s"], 1)
                nc.scalar.activation(LT[:, 3], ZS[:, :, 16:32], ACT.Exp, scale=-1.0).then_inc(S["gate_s"], 1)
                act.wait_ge(S["gate_v"], at(g * 6 + 4))
                act.wait_ge(S["gate_s"], at(g * 3 + 1))
                nc.scalar.activation(LT[:, 0], LT[:, 2], ACT.Ln).then_inc(S["gate_s"], 1)
                for p in range(NP):
                    for n, src in enumerate((GR, CH, BD, SP)):
                        act.wait_ge(S["dec_mm"], at(g * 16 + 4 * p + n + 1))
                        act.wait_ge(S["x3_done"], at(g * 2))
                        dst = (EA if n < 2 else EQ)[:, (n % 2) * 8:(n % 2) * 8 + 8, p, :]
                        nc.scalar.activation(dst, src[:, :].rearrange("p (h t) -> p h t", h=8), ACT.Exp).then_inc(S["dec_exp"], 1)
                it0 = g * NH
                tap(it0, 0)
                tap(it0, 1)
                silu_kq(it0, 0)
                tap(it0, 2)
                silu_kq(it0, 1)
                tap(it0, 3)
                silu_v(it0, 2)
                silu_v(it0, 3)

                def levels(j, i):
                    x_diag(j, 1)
                    if i is not None:
                        tap(i, 0)
                    x_diag(j, 2)
                    if i is not None:
                        tap(i, 1)
                    x_diag(j, 3)
                    if i is not None:
                        silu_kq(i, 0)
                        tap(i, 2)
                    x_diag(j, 4)
                    if i is not None:
                        silu_kq(i, 1)
                        tap(i, 3)
                    x_diag(j, 5)
                    x_diag(j, 6)
                    o_out(j)
                    if i is not None:
                        silu_v(i, 2)
                        silu_v(i, 3)

                with act.Fori(1, NH) as h:
                    levels(g * NH + h - 1, g * NH + h)
                levels(g * NH + NH - 1, None)

                transposed(g * 3 + 1, 1)
                for p in range(NP):
                    pid = g * NP + p
                    for r in range(4):
                        act.wait_ge(S["sub_done"], at(pid * 4 + r + 1))
                        nc.scalar.activation(ES[:, :, r], ES[:, :, r], ACT.Exp, scale=float(D8) ** -0.5).then_inc(S["exp_done"], 1)
                    for r in range(4):
                        act.wait_ge(S["pt_mm"], at(pid * 4 + r + 1))
                        act.wait_ge(S["pv_mm"], at(pid))
                        nc.scalar.activation(PT[:, r], PJ[r % 2][:, :].rearrange("p (q s) -> p q s", q=4), ACT.Copy).then_inc(S["pt_done"], 1)
                transposed(g * 3 + 2, 2)
                for f in range(FB):
                    act.wait_ge(S["f1_mm"], at(g * FB + f + 1))
                    nc.scalar.activation(H[:, f, :], (GR, CH, BD, SP)[f % 4][:, :], ACT.Gelu, bias=B1[:, f:f + 1]).then_inc(S["gelu_done"], 1)

        @block.vector
        def _(dve):
            start_counts(dve, "dve")
            V_ = nc.vector
            for n in range(8):
                dve.wait_ge(S["w_hi"], n + 1)
                sl = slice((n % 4) * 2048, (n % 4 + 1) * 2048)
                V_.scalar_tensor_tensor(WL[:, n // 4, sl], SCR[:, sl], WS, WH[:, n // 4, sl], ALU.mult, ALU.subtract).then_inc(S["w_split"], 1)
            dve.wait_ge(S["ld_const"], 96)
            V_.tensor_copy(ABH[:, :, :], AB32[:, :, :]).then_inc(S["conv_scaled"], 1)
            cwv = CW[:, :, :].rearrange("p h (b n) -> p (h b) n", n=5)[:, :, 0:4]
            V_.tensor_scalar(cwv, cwv, 1.0 / WS, None, ALU.mult).then_inc(S["conv_scaled"], 1)
            dve.wait_ge(S["conv_scaled"], 2)
            V_.tensor_tensor(ABL[:, :, :], AB32[:, :, :], ABH[:, :, :], ALU.subtract).then_inc(S["conv_scaled"], 1)
            for m in (A, X, M):
                V_.memset(m[:, :, :], 0.0).then_inc(S["conv_scaled"], 1)
            V_.memset(ONES[:, :], 1.0).then_inc(S["conv_scaled"], 1)
            V_.memset(ZW[:, :], 0.0).then_inc(S["conv_scaled"], 1)
            V_.memset(XH[:, :, GT:GT + 1], 0.0).then_inc(S["conv_scaled"], 1)
            V_.memset(XL[:, :, GT:GT + 1], 0.0).then_inc(S["conv_scaled"], 1)
            dve.wait_ge(LW[0], 48)
            dve.wait_ge(LW[1], 48)
            for n in range(2):
                V_.tensor_reduce(SMALL[:, n:n + 1], SCR[:, 2048 * n:2048 * n + 2048], AX_X, ALU.add,
                                 apply_absolute_value=True).then_inc(S["tern_sum"], 1)
            dve.wait_ge(S["tern_all"], 1)
            V_.tensor_scalar(SMALL[:, 4:6], SMALL[:, 2:4], 1.0 / (E * F), 1e-8, ALU.mult, ALU.max).then_inc(S["tern_done"], 1)
            dve.wait_ge(S["tern_done"], 1)
            V_.tensor_scalar(SMALL[:, 6:8], SMALL[:, 4:6], -0.5, None, ALU.mult).then_inc(S["tern_done"], 1)
            V_.tensor_scalar(SMALL[:, 0:2], SMALL[:, 4:6], 0.5, None, ALU.mult).then_inc(S["tern_done"], 1)
            dve.wait_ge(S["tern_done"], 3)
            for n, dst in enumerate((W1[:, :, :].rearrange("p c f -> p (c f)"), W2[:, :, :].rearrange("p f e -> p (f e)"))):
                w = SCR[:, 2048 * n:2048 * n + 2048]
                V_.tensor_scalar(SCR[:, 4096 + 2048 * n:6144 + 2048 * n], w, SMALL[:, 6 + n:7 + n], None, ALU.is_lt).then_inc(S["tern_done"], 1)
                dve.wait_ge(S["tern_done"], 4 + 2 * n)
                V_.scalar_tensor_tensor(dst, w, SMALL[:, n:n + 1], SCR[:, 4096 + 2048 * n:6144 + 2048 * n], ALU.is_gt, ALU.subtract).then_inc(S["tern_done"], 1)

            def norm(nid, src):
                dve.wait_ge(S["ln_step"], at(nid * 13))
                for p in range(NP):
                    V_.bn_stats(STT6[:, p, :], src[:, p, :]).then_inc(S["ln_step"], 1)
                dve.wait_ge(S["ln_step"], at(nid * 13 + 4))
                dve.nop(nofuse=True)
                for p in range(NP):
                    V_.bn_aggr(MV[:, p, :], STT6[:, p, :]).then_inc(S["ln_step"], 1)
                dve.wait_ge(S["ln_step"], at(nid * 13 + 8))
                V_.tensor_scalar(VE[:, :], MV[:, :, 1], 1e-5, None, ALU.add).then_inc(S["ln_step"], 1)
                dve.wait_ge(S["rstd"], at(nid + 1))
                dve.wait_ge(S["tr_done"], at(nid * 2))
                for p in range(NP):
                    V_.tensor_scalar(XN[:, p, :], src[:, p, :], MV[:, p, 0:1], RSTD[:, p:p + 1], ALU.subtract, ALU.mult).then_inc(S["ln_step"], 1)

            def low_parts(nid, lid):
                for c in range(2):
                    dve.wait_ge(S["xh_done"], at(nid * 2 + c + 1))
                    V_.tensor_tensor(XL[:, c, 0:GT], PJ[c][:, :], XH[:, c, 0:GT], ALU.subtract).then_inc(S["xl_done"], 1)

            def cw_cur(it, h):
                dve.wait_ge(S["tap"], at(it * 4))
                dve.wait_ge(S["conv"], at(it * 12))
                V_.tensor_copy(CWC[:, :], CW[:, ds(h, 1), :].rearrange("p o n -> p (o n)")).then_inc(S["cw_cur"], 1)
                dve.wait_ge(S["cw_cur"], at(it + 1))

            def conv(it, b, m):
                if m == 1:
                    dve.wait_ge(S["tap"], at(it * 4 + b + 1))
                else:
                    dve.wait_ge(S["conv"], at(it * 12 + 3 * b + m - 1))
                yv = Y[:, b, :].rearrange("p (n t) -> p n t", t=T)
                pv = PJ[b % 2][:, :].rearrange("p (n t) -> p n t", t=T)
                V_.scalar_tensor_tensor(yv[:, :, m:T], pv[:, :, 0:T - m], CWC[:, 5 * b + 3 - m:5 * b + 4 - m], yv[:, :, m:T],
                                        ALU.mult, ALU.add).then_inc(S["conv"], 1)

            def prepare(j, h):
                dve.wait_ge(S["ss_mm"], at(j + 1))
                ss = CH[:, 0:8]
                V_.tensor_scalar(SSM[:, :], ss, 1e-24, None, ALU.max).then_inc(S["scale_done"], 1)
                dve.wait_ge(S["rsq"], at(j + 1))
                dve.wait_ge(S["t1_done"], at(j))
                V_.tensor_tensor(NBT[:, :], NQ[:, 0, :], BE[:, ds(h, 1), :].rearrange("p o a -> p (o a)"), ALU.mult).then_inc(S["scale_done"], 1)
                dve.wait_ge(S["r_mm"], at(j))
                V_.tensor_tensor(DQ[:, :, :], over_pairs(identc), NQ[:, 1, :][:, :, None].broadcast_to([P, NP, T]), ALU.mult).then_inc(S["dq_done"], 1)
                dve.wait_ge(S["scale_done"], at(j * 4 + 2))
                V_.tensor_tensor(RA[:, :], NBT[:, :], NQ[:, 0, :], ALU.mult).then_inc(S["scale_done"], 1)
                dve.wait_ge(S["scale_done"], at(j * 4 + 3))
                dve.wait_ge(S["masked"], at(j * 2 + 2))
                dve.wait_ge(S["a_done"], at(j * 2))
                V_.tensor_tensor(EAR[:, :, :], EAM[:, :, :], RA[:, :][:, :, None].broadcast_to([P, NP, T]), ALU.mult).then_inc(S["scale_done"], 1)
                dve.wait_ge(S["scale_done"], at(j * 4 + 4))
                dve.wait_ge(S["gram_mm"], at(j + 1))
                dve.wait_ge(S["w_mm"], at(j * LV))
                for n in range(2):
                    lo = 64 * n
                    V_.tensor_tensor(A[lo:lo + 64, :, lo:lo + 64], gram[lo:lo + 64, :, 0, :], EAR[lo:lo + 64, :, :], ALU.mult).then_inc(S["a_done"], 1)
                dve.wait_ge(S["m_mm"], at(j))
                V_.tensor_tensor(GQ[:, :, :], gram[:, :, 1, :], EQM[:, :, :], ALU.mult).then_inc(S["gq_done"], 1)
                dve.wait_ge(S["r_mm"], at(j + 1))
                dve.wait_ge(S["m_done"], at(j * 2))
                V_.tensor_tensor(T1[:, :, :], psR, NBT[:, :][:, :, None].broadcast_to([P, NP, T]), ALU.mult).then_inc(S["t1_done"], 1)

            def w_masked(j, k):
                dve.wait_ge(S["w_mm"], at(j * LV + k + 1))
                if k == 0:
                    dve.wait_ge(S["p_mm"], at(j * 5))
                V_.tensor_tensor(W[:, :, :], psW, over_pairs(mt(k)), ALU.mult).then_inc(S["w_done_v"], 1)

            def z_next(j, k):
                if k == 0:
                    dve.wait_ge(S["w_done_v"], at(j * LV + 1))
                    dve.wait_ge(S["t_mm"], at(j * LV))
                    V_.tensor_tensor(Z[:, :, :], over_pairs(identc), W[:, :, :], ALU.subtract).then_inc(S["z_done"], 1)
                else:
                    dve.wait_ge(S["z_done"], at(j * LV + k))
                    dve.wait_ge(S["p_mm"], at(j * 5 + k))
                    V_.tensor_tensor(Z[:, :, :], Z[:, :, :], psP, ALU.subtract).then_inc(S["z_done"], 1)

            def m_diag(j):
                dve.wait_ge(S["m_mm"], at(j + 1))
                dve.wait_ge(S["t1_done"], at(j + 1))
                dve.wait_ge(S["o_mm"], at(j * 2))
                for n in range(2):
                    lo = 64 * n
                    V_.tensor_tensor(M[lo:lo + 64, :, lo:lo + 64], psW[lo:lo + 64], T1[lo:lo + 64, :, :], ALU.mult).then_inc(S["m_done"], 1)

            with dve.Fori(0, G) as g:
                dve.wait_ge(S["ld_x"], at(g * 16 + 16))
                norm(g * 3, XP)
                low_parts(g * 3, 0)
                dve.wait_ge(S["gate_mm"], at(g + 1))
                dve.wait_ge(S["gate_v"], at(g * 6))
                V_.tensor_copy(ZS[:, :, :], SP[:, 0:128].rearrange("p (a n) -> p a n", a=NP)).then_inc(S["gate_v"], 1)
                dve.wait_ge(S["gate_v"], at(g * 6 + 1))
                V_.scalar_tensor_tensor(LT[:, 0], ZS[:, :, 0:16], -1.0, ZS[:, :, 0:16], ALU.mult, ALU.max).then_inc(S["gate_v"], 1)
                V_.tensor_scalar(LT[:, 1], ZS[:, :, 0:16], 0.0, None, ALU.min).then_inc(S["gate_v"], 1)
                dve.wait_ge(S["gate_s"], at(g * 3 + 2))
                V_.tensor_scalar(LT[:, 2:4], LT[:, 2:4], 1.0, None, ALU.add).then_inc(S["gate_v"], 1)
                dve.wait_ge(S["gate_v"], at(g * 6 + 4))
                V_.reciprocal(BE[:, :, :].rearrange("p h a -> p a h"), LT[:, 3]).then_inc(S["gate_v"], 1)
                dve.wait_ge(S["gate_s"], at(g * 3 + 3))
                dve.wait_ge(S["rha_done"], at(g * NP))
                V_.tensor_tensor(LA[:, :, :], LT[:, 1], LT[:, 0], ALU.subtract).then_inc(S["gate_v"], 1)
                dve.wait_ge(S["gate_v"], at(g * 6 + 6))
                for p in range(NP):
                    if p:
                        dve.wait_ge(S["dec_mm"], at(g * 16 + 4 * p - 2))
                    V_.tensor_tensor(RHA, CST[:, C_LEC:C_LEC + 64][:, None, :].broadcast_to([P, NH, T]),
                                     LA[:, p, :][:, :, None].broadcast_to([P, NH, T]), ALU.mult).then_inc(S["rha_done"], 1)

                it0 = g * NH
                cw_cur(it0, 0)
                for b in range(4):
                    for m in (1, 2, 3):
                        conv(it0, b, m)

                def levels(j, hj, i, hi):
                    if i is not None:
                        cw_cur(i, hi)
                    prepare(j, hj)
                    w_masked(j, 0)
                    z_next(j, 0)
                    for k in range(1, LV):
                        w_masked(j, k)
                        if i is not None and k >= 2:
                            conv(i, k - 2, 1)
                        z_next(j, k)
                        if i is not None and k >= 2:
                            conv(i, k - 2, 2)
                            conv(i, k - 2, 3)
                    m_diag(j)

                with dve.Fori(1, NH) as h:
                    levels(g * NH + h - 1, h - 1, g * NH + h, h)
                levels(g * NH + NH - 1, NH - 1, None, None)

                dve.wait_ge(S["op_mm"], at(g * NH + NH))
                dve.wait_ge(S["x_copied"], at(g + 1))
                for n in range(2):
                    xv = XC[:, 2 * n:2 * n + 2, :].rearrange("p a e -> p (a e)")
                    V_.tensor_tensor(xv, AC[n][:, :], xv, ALU.add).then_inc(S["x1_done"], 1)
                dve.wait_ge(S["x1_done"], at(g * 2 + 2))
                norm(g * 3 + 1, XC)
                for c, src in enumerate((GR, CH)):
                    dve.wait_ge(S["rep_mm"], at(g * 2 + c + 1))
                    for b in range(8):
                        ins = V_.tensor_tensor(KG[:, c, b], src[:, T * b:T * b + T][:, None, :].broadcast_to([P, 4, T]),
                                               CST[:, C_GM:C_GM + 4][:, :, None].broadcast_to([P, 4, T]), ALU.mult)
                    ins.then_inc(S["kg_done"], 1)

                def softmax_in(p):
                    pid = g * NP + p
                    for r, src in enumerate((GR, CH, BD, SP)):
                        sv = src[:, :].rearrange("p (c g t) -> p c g t", c=2, g=4)
                        dve.wait_ge(S["sc_mm"], at(pid * 4 + r + 1))
                        dve.wait_ge(S["sub_done"], at(pid * 4 + r))
                        V_.tensor_reduce(MX[:, r, :], src[:, :].rearrange("p (n t) -> p n t", t=T), AX_X, ALU.max).then_inc(S["mx_done"], 1)
                        dve.wait_ge(S["mx_done"], at(pid * 4 + r + 1))
                        if r == 0:
                            dve.wait_ge(S["pt_mm"], at(pid * 4))
                        V_.tensor_tensor(ES[:, :, r], sv, MX[:, r, :].rearrange("p (c g) -> p c g", c=2)[:, :, :, None].broadcast_to([P, 2, 4, T]),
                                         ALU.subtract).then_inc(S["sub_done"], 1)

                def softmax_out(p):
                    pid = g * NP + p
                    pv = AC[p % 2][:, 0:288].rearrange("p (n d) -> p n d", d=9)
                    dve.wait_ge(S["pv_mm"], at(pid + 1))
                    dve.wait_ge(S["ob_done"], at(pid))
                    V_.reciprocal(RS[:, :], pv[:, :, 8]).then_inc(S["rs_done"], 1)
                    dve.wait_ge(S["rs_done"], at(pid + 1))
                    dve.wait_ge(S["nrm_done"], at(pid))
                    V_.tensor_tensor(OB[:, :, :], pv[:, :, 0:8], RS[:, :][:, :, None].broadcast_to([P, 32, D8]), ALU.mult).then_inc(S["ob_done"], 1)
                    dve.wait_ge(S["ob_done"], at(pid + 1))
                    V_.tensor_tensor(XC[:, p, :], XC[:, p, :], OB[:, :, :].rearrange("p n d -> p (n d)"), ALU.add).then_inc(S["nrm_done"], 1)

                for p in range(NP):
                    softmax_in(p)
                    if p:
                        softmax_out(p - 1)
                softmax_out(NP - 1)
                dve.wait_ge(S["nrm_done"], at(g * NP + NP))
                norm(g * 3 + 2, XC)
                low_parts(g * 3 + 2, 1)
                for f in range(FB):
                    dve.wait_ge(S["gelu_done"], at(g * FB + f + 1))
                    V_.tensor_copy(HH[:, f, :], H[:, f, :]).then_inc(S["hh_done"], 1)
                    dve.wait_ge(S["hh_done"], at(g * FB + f + 1))
                    V_.tensor_tensor(HL[:, f, :], H[:, f, :], HH[:, f, :], ALU.subtract).then_inc(S["hl_done"], 1)
                dve.wait_ge(S["f2_mm"], at(g + 1))
                for n in range(2):
                    xv = XC[:, 2 * n:2 * n + 2, :]
                    V_.tensor_tensor(xv, AC[n][:, :].rearrange("p (a e) -> p a e", a=2), xv, ALU.add).then_inc(S["y_done"], 1)
                dve.wait_ge(S["y_done"], at(g * 2 + 2))
                for n in range(2):
                    xv = XC[:, 2 * n:2 * n + 2, :]
                    V_.tensor_tensor(xv, xv, B2[:, :][:, None, :].broadcast_to([P, 2, E]), ALU.add).then_inc(S["x3_done"], 1)

        @block.tensor
        def _(pe):
            start_counts(pe, "pe")
            mm = nc.tensor.matmul
            pe.wait_ge(S["ld_const"], 96)
            pe.wait_ge(S["conv_scaled"], 10)
            pe.wait_ge(S["tern_done"], 7)
            pe.wait_ge(S["zeroed"], 4)
            pe.wait_ge(S["w_hi"], 8)

            def transposes(nid):
                pe.wait_ge(S["ln_step"], at(nid * 13 + 13))
                for c in range(2):
                    for p in range(NP):
                        ins = nc.tensor.transpose(PJ[c][:, P * p:P * p + P], XN[:, p, P * c:P * c + P], ident)
                    ins.then_inc(S["tr_done"], 1)

            TERMS = [(WH, XH), (WH, XL), (WL, XH)]

            def project(it, h, b):
                if b >= 2:
                    pe.wait_ge(S["conv"], at(it * 12 + 3 * b - 3))
                else:
                    pe.wait_ge(S["conv"], at(it * 12))
                n = 0
                for c in range(2):
                    for wt, xt in TERMS:
                        ins = mm(PJ[b % 2][:, :], wt[:, c, ds(h * 512 + b * P, P)], xt[:, c, 0:GT], start=(n == 0), stop=(n == 5))
                        n += 1
                ins.then_inc(S["proj"], 1)

            def grams(j):
                pe.wait_ge(S["kq"], at(j * 2 + 2))
                pe.wait_ge(S["ot_done"], at(j * 2))
                for p in range(NP):
                    for n in range(2):
                        c0 = P * p + 64 * n
                        ins = mm(gram[64 * n:64 * n + 64, p], KQ[:, 0, c0:c0 + 64], KQ[:, :, c0:c0 + 64], start=True, stop=True)
                ins.then_inc(S["gram_mm"], 1)
                pe.wait_ge(S["sq"], at(j * 2 + 2))
                pe.wait_ge(S["v_done"], at(j * 2 + 2))
                for a in range(2):
                    for p in range(NP):
                        ins = mm(CH[:, a * NP + p:a * NP + p + 1], SQ[:, a, P * p:P * p + P], ONES[:, :], start=True, stop=True)
                ins.then_inc(S["ss_mm"], 1)

            def spread_q(j):
                pe.wait_ge(S["dq_done"], at(j + 1))
                mm(BD[:, 0:256], CST[:, C_ON:C_ON + 128], DQ[:, :, :].rearrange("p a t -> p (a t)"), start=True, stop=True).then_inc(S["r_mm"], 1)

            def w_level(j, k):
                if k == 0:
                    pe.wait_ge(S["a_done"], at(j * 2 + 2))
                else:
                    pe.wait_ge(S["z_done"], at(j * LV + k))
                for p in range(NP):
                    ins = mm(psW[:, p], A[:, p, :], identc if k == 0 else Z[:, p, :], start=True, stop=True)
                ins.then_inc(S["w_mm"], 1)

            def t_level(j, k):
                pe.wait_ge(S["z_done"], at(j * LV + k))
                if k == 1:
                    pe.wait_ge(S["t1_done"], at(j + 1))
                else:
                    pe.wait_ge(S["x_bd"], at(j * 12 + 2 * (k - 1)))
                pe.nop(nofuse=True)
                for p in range(NP):
                    ins = nc.tensor.transpose(psX[0:64, p], Z[:, p, :], ident)
                ins.then_inc(S["t_mm"], 1)

            def p_level(j, k):
                pe.wait_ge(S["w_done_v"], at(j * LV + k + 1))
                pe.wait_ge(S["x_bd"], at(j * 12 + 2 * k))
                for p in range(NP):
                    ins = mm(psP[:, p], X[:, p, :], W[:, p, :], start=True, stop=True)
                ins.then_inc(S["p_mm"], 1)

            def m_level(j):
                pe.wait_ge(S["x_bd"], at(j * 12 + 12))
                pe.wait_ge(S["gq_done"], at(j + 1))
                for p in range(NP):
                    ins = mm(psW[:, p], X[:, p, :], GQ[:, p, :], start=True, stop=True)
                ins.then_inc(S["m_mm"], 1)

            def outputs(j):
                pe.wait_ge(S["m_done"], at(j * 2 + 2))
                pe.wait_ge(S["v_done"], at(j * 2 + 2))
                for n, dst in enumerate((GR, BD)):
                    for p in range(NP):
                        ins = mm(dst[:, P * p:P * p + P], V[:, p, P * n:P * n + P], M[:, p, :], start=True, stop=True)
                    ins.then_inc(S["o_mm"], 1)

            def v_transposes(i):
                for n, dst in enumerate((SP, CH)):
                    pe.wait_ge(S["conv"], at(i * 12 + 9 + 3 * n))
                    if n == 0:
                        pe.wait_ge(S["v_done"], at(i * 2))
                    for p in range(NP):
                        ins = nc.tensor.transpose(dst[:, P * p:P * p + P], Y[:, 2 + n, P * p:P * p + P], ident)
                    ins.then_inc(S["vt_mm"], 1)

            def project_out(j, h, last):
                pe.wait_ge(S["ot_done"], at(j * 2 + 2))
                for p in range(NP):
                    for n in range(2):
                        ins = mm(AC[p // 2][:, E * (p % 2):E * (p % 2) + E], OT[:, n, P * p:P * p + P],
                                 WO[:, ds(h * 2 + n, 1), :].rearrange("p o e -> p (o e)"), start=False, stop=(last and n == 1), skip_group_check=True)
                ins.then_inc(S["op_mm"], 1)

            with pe.Fori(0, G) as g:
                transposes(g * 3)
                pe.wait_ge(S["xl_done"], at(g * 4 + 2))
                for p in range(NP):
                    for n in range(2):
                        k = 0
                        for c in range(2):
                            for xt, wt in ((XH, ABH), (XL, ABH), (XH, ABL)):
                                o = P * p + 1 - n
                                ins = mm(SP[:, 32 * p + 16 * n:32 * p + 16 * n + 16], xt[:, c, o:o + P], wt[:, c, 16 * n:16 * n + 16],
                                         start=(k == 0), stop=(k == 5))
                                k += 1
                ins.then_inc(S["gate_mm"], 1)
                for p in range(NP):
                    pe.wait_ge(S["rha_done"], at(g * NP + p + 1))
                    if p:
                        pe.wait_ge(S["dec_exp"], at(g * 16 + 4 * p - 2))
                    for n, dst in enumerate((GR, CH)):
                        mm(dst[:, :], CST[:, C_UT:C_UT + 128], RHA[:, 8 * n:8 * n + 8, :].rearrange("p a t -> p (a t)"),
                           start=True, stop=True).then_inc(S["dec_mm"], 1)
                    pe.wait_ge(S["rhq_done"], at(g * NP + p + 1))
                    if p:
                        pe.wait_ge(S["dec_exp"], at(g * 16 + 4 * p))
                    for n, dst in enumerate((BD, SP)):
                        mm(dst[:, :], CST[:, C_LE:C_LE + 128], RHQ[:, 8 * n:8 * n + 8, :].rearrange("p a t -> p (a t)"),
                           start=True, stop=True).then_inc(S["dec_mm"], 1)
                for n in range(2):
                    mm(AC[n][:, :], ZW[:, :], XH[:, 0, 0:GT], start=True, stop=False, skip_group_check=True)
                it0 = g * NH
                pe.wait_ge(S["dec_exp"], at(g * 16 + 16))
                for b in range(4):
                    project(it0, 0, b)
                v_transposes(it0)

                def levels(j, hj, i, hi, last):
                    grams(j)
                    if i is not None:
                        project(i, hi, 0)
                    spread_q(j)
                    w_level(j, 0)
                    for k in range(1, LV):
                        w_level(j, k)
                        t_level(j, k)
                        if i is not None and 2 <= k <= 4:
                            project(i, hi, k - 1)
                        p_level(j, k)
                    t_level(j, LV)
                    m_level(j)
                    outputs(j)
                    if i is not None:
                        v_transposes(i)
                    project_out(j, hj, last)

                with pe.Fori(1, NH) as h:
                    levels(g * NH + h - 1, h - 1, g * NH + h, h, False)
                levels(g * NH + NH - 1, NH - 1, None, None, True)

                pe.wait_ge(S["ld_ctx"], at(g * 48 + 48))
                for c, dst in enumerate((GR, CH)):
                    mm(dst[:, :], CST[0:64, C_REP + 128 * c:C_REP + 128 * c + 128], CT[:, :], start=True, stop=True).then_inc(S["rep_mm"], 1)
                transposes(g * 3 + 1)
                pe.wait_ge(S["xh_done"], at(g * 6 + 4))
                pe.wait_ge(S["kg_done"], at(g * 2 + 2))
                pe.wait_ge(S["vb_done"], at(g * 2 + 2))

                def scores(p):
                    pid = g * NP + p
                    for r, dst in enumerate((GR, CH, BD, SP)):
                        if p:
                            pe.wait_ge(S["sub_done"], at(pid * 4 + r - 3))
                        for c in range(2):
                            for n in range(2):
                                b = 2 * p + n
                                ins = mm(dst[64 * n:64 * n + 64, 256 * c:256 * c + 256], QT[32 * r:32 * r + 32, c, T * b:T * b + T],
                                         KG[32 * r:32 * r + 32, c, b].rearrange("p g t -> p (g t)"), start=True, stop=True, tile_position=(32 * r, 64 * n))
                        ins.then_inc(S["sc_mm"], 1)

                scores(0)
                for p in range(NP):
                    pid = g * NP + p
                    for r in range(4):
                        pe.wait_ge(S["exp_done"], at(pid * 4 + r + 1))
                        if r >= 2:
                            pe.wait_ge(S["pt_done"], at(pid * 4 + r - 1))
                        else:
                            pe.wait_ge(S["pt_done"], at(pid * 4))
                        for q in range(4):
                            ins = nc.tensor.transpose(PJ[r % 2][:, P * q:P * q + P], ES[:, q // 2, r, 2 * (q % 2):2 * (q % 2) + 2, :], ident)
                        ins.then_inc(S["pt_mm"], 1)
                    if p + 1 < NP:
                        scores(p + 1)
                    pe.wait_ge(S["pt_done"], at(pid * 4 + 4))
                    if p >= 2:
                        pe.wait_ge(S["nrm_done"], at(pid - 1))
                    for r in range(4):
                        for q in range(4):
                            kv = 4 * (q // 2) + r
                            for n in range(2):
                                b = 2 * p + n
                                col = (2 * kv + q % 2) * 18
                                ins = mm(AC[p % 2][64 * n:64 * n + 64, col:col + 18], PT[:, r, q, 64 * n:64 * n + 64],
                                         VB[:, 8 * b + kv].rearrange("p g d -> p (g d)"), start=True, stop=True)
                    ins.then_inc(S["pv_mm"], 1)

                transposes(g * 3 + 2)
                pe.wait_ge(S["xl_done"], at(g * 4 + 4))
                for f in range(FB):
                    if f >= 4:
                        pe.wait_ge(S["gelu_done"], at(g * FB + f - 3))
                    k = 0
                    for c in range(2):
                        for xt in (XH, XL):
                            ins = mm((GR, CH, BD, SP)[f % 4][:, :], W1[:, c, P * f:P * f + P], xt[:, c, 0:GT], start=(k == 0), stop=(k == 3))
                            k += 1
                    ins.then_inc(S["f1_mm"], 1)
                for f in range(FB):
                    pe.wait_ge(S["hl_done"], at(g * FB + f + 1))
                    for p in range(NP):
                        for k, ht in enumerate((HH, HL)):
                            ins = mm(AC[p // 2][:, E * (p % 2):E * (p % 2) + E], ht[:, f, P * p:P * p + P], W2[:, f, :],
                                     start=(f == 0 and k == 0 and p % 2 == 0), stop=(f == FB - 1 and k == 1), skip_group_check=True)
                ins.then_inc(S["f2_mm"], 1)


_NAMES = ["x", "ctxT", "ctxR", "wall", "wo", "wab", "cw", "w1", "b1", "w2", "b2", "cst"]


def kernel(**inp):
    import numpy as _np
    import concourse.bacc as _bacc
    from concourse import mybir as _mybir
    from concourse.bass_utils import run_bass_kernel_spmd as _run

    a = {k: _np.asarray(v) for k, v in inp.items()}
    x = a["x"].reshape(G, NP, P, E).transpose(0, 2, 1, 3)
    c = a["ctx_512"]
    ctxT = c.reshape(G, 8 * T, CD).transpose(0, 2, 1)
    ctxR = c.reshape(G, 8, T, CD).transpose(0, 2, 1, 3)
    wq = a["L0_attn_Wq"].reshape(E, NH, DK)
    wk = a["L0_attn_Wk"].reshape(E, NH, DK)
    wv = a["L0_attn_Wv"].reshape(E, NH, 2 * DK)
    wall = _np.concatenate([wq, wk, wv], axis=2).reshape(2, P, NH * 512)
    wo = a["L0_attn_Wo"].reshape(2 * NH, P, E).transpose(1, 0, 2)
    wab = _np.concatenate([a["L0_attn_Wa"], a["L0_attn_Wb"]], axis=1).reshape(2, P, 32).transpose(1, 0, 2)

    def taps(w, b, n):
        return _np.concatenate([w, b[:, None]], axis=1).reshape(NH, n, P, 5)

    cw = _np.concatenate([taps(a["L0_attn_qcw"], a["L0_attn_qcb"], 1), taps(a["L0_attn_kcw"], a["L0_attn_kcb"], 1),
                          taps(a["L0_attn_vcw"], a["L0_attn_vcb"], 2)], axis=1).transpose(2, 0, 1, 3).reshape(P, NH, 20)
    w1 = a["L0_ffn_w1"].T.reshape(2, P, F).transpose(1, 0, 2).reshape(P, 2 * F)
    w2 = a["L0_ffn_w2"].T.reshape(FB, P, E).transpose(1, 0, 2).reshape(P, FB * E)
    b1 = a["L0_ffn_b1"].reshape(FB, P).T
    b2 = _np.broadcast_to(a["L0_ffn_b2"][None, :], (P, E))
    vals = dict(x=x, ctxT=ctxT, ctxR=ctxR, wall=wall, wo=wo, wab=wab, cw=cw, w1=w1, b1=b1, w2=w2, b2=b2, cst=constants())

    nc = _bacc.Bacc("TRN2", target_bir_lowering=False, num_devices=1)
    arrays, args = {}, []
    for name in _NAMES:
        v = _np.ascontiguousarray(vals[name])
        arrays[f"in_{name}"] = v
        args.append(nc.dram_tensor(f"in_{name}", v.shape, _mybir.dt.from_np(v.dtype), kind="ExternalInput").ap())
    out = nc.dram_tensor("out", (G, P, NP, E), _mybir.dt.float32, kind="ExternalOutput").ap()
    build(nc, *args, out)
    r = _run(nc, [arrays], core_ids=[0])
    y = r.results[0]["out"]
    return y.transpose(0, 2, 1, 3).reshape(NB, T, E)
```

```python
from contextlib import ExitStack

import numpy as np
import concourse.bass as bass
from concourse import mybir

ALU = mybir.AluOpType
ACT = mybir.ActivationFunctionType
F32 = mybir.dt.float32
F16 = mybir.dt.float16
AX_X = mybir.AxisListType.X
ds = bass.ds

P = 128
T = 64
E = 256
NB = 64
GT = 512
G = NB * T // GT
NP = GT // P
NH = 16
DK = 128
LV = 6
CD = 64
F = 1024
FB = F // P
WS = 64.0
D8 = 8

C_ID, C_IC, C_MT = 0, 128, 192
C_UT, C_LE, C_ON = C_MT + 64 * LV, C_MT + 64 * LV + 128, C_MT + 64 * LV + 256
C_UTC = C_ON + 128
C_LEC, C_MA, C_MQ = C_UTC + 64, C_UTC + 128, C_UTC + 192
C_REP = C_MQ + 64
C_GM = C_REP + 256
NCST = C_GM + 4


def constants():
    c = np.zeros((P, NCST), np.float32)
    p = np.arange(P)[:, None]
    q = np.arange(P)[None, :]
    s, j = p % T, np.arange(T)[None, :]
    same = (p // T) == (q // T)
    c[:, C_ID:C_ID + 128] = p == q
    c[:, C_IC:C_IC + 64] = s == j
    for k in range(LV):
        c[:, C_MT + 64 * k:C_MT + 64 * k + 64] = ((s >> (k + 1)) == (j >> (k + 1))) & ((s >> k) % 2 == 0) & ((j >> k) % 2 == 1)
    c[:, C_UT:C_UT + 128] = same & (p < q)
    c[:, C_LE:C_LE + 128] = same & (p >= q)
    c[:, C_ON:C_ON + 128] = same
    c[:, C_UTC:C_UTC + 64] = s < j
    c[:, C_LEC:C_LEC + 64] = s >= j
    c[:, C_MA:C_MA + 64] = s > j
    c[:, C_MQ:C_MQ + 64] = s <= j
    for half in range(2):
        for m in range(P):
            c[(half * 4 + m // 32) * D8 + m % D8, C_REP + 128 * half + m] = 1.0
    c[:, C_GM:C_GM + 4] = (p // D8) % 4 == np.arange(4)[None, :]
    return c


def build(nc, x, ctxT, ctxR, wall, wo, wab, cw, w1, b1, w2, b2, cst, out):
    ctx = ExitStack()
    with ctx:
        def sb(name, shape, dt=F32):
            return ctx.enter_context(nc.sbuf_tensor(name, shape, dt))

        def sem(name):
            return ctx.enter_context(nc.semaphore(name))

        WH = sb("WH", [P, 2, NH * 512], F16)
        WL = sb("WL", [P, 2, NH * 512], F16)
        WO = sb("WO", [P, 2 * NH, E])
        SCR = sb("SCR", [P, 8192])
        CST = sb("CST", [P, NCST])
        CW = sb("CW", [P, NH, 20])
        CWC = sb("CWC", [P, 20])
        AB32 = sb("AB32", [P, 2, 32])
        ABH = sb("ABH", [P, 2, 32], F16)
        ABL = sb("ABL", [P, 2, 32], F16)
        W1 = sb("W1", [P, 2, F], F16)
        W2 = sb("W2", [P, FB, E], F16)
        B1 = sb("B1", [P, FB])
        B2 = sb("B2", [P, E])
        XP = sb("XP", [P, NP, E])
        XC = sb("XC", [P, NP, E])
        XH = sb("XH", [P, 2, GT + 1], F16)
        XL = sb("XL", [P, 2, GT + 1], F16)
        STT6 = sb("STT6", [P, NP, 6])
        MV = sb("MV", [P, NP, 2])
        RSTD = sb("RSTD", [P, NP])
        VE = sb("VE", [P, NP])
        SSM = sb("SSM", [P, 2 * NP])
        MHALF = sb("MHALF", [P, 2 * NP])
        LA = sb("LA", [P, NP, NH])
        LT = sb("LT", [P, 4, NP, NH])
        BE = sb("BE", [P, NH, NP])
        KQ = sb("KQ", [P, 2, GT])
        Y = sb("Y", [P, 4, GT])
        V = sb("V", [P, NP, 256])
        SQ = sb("SQ", [P, 2, GT])
        XN = SQ[:, :, :].rearrange("p a (b e) -> p (a b) e", e=E)
        NQ = sb("NQ", [P, 2, NP])
        NBT = sb("NBT", [P, NP])
        RA = sb("RA", [P, NP])
        EAM = sb("EAM", [P, NP, T])
        EQM = sb("EQM", [P, NP, T])
        EAR = sb("EAR", [P, NP, T])
        A = sb("A", [P, NP, P])
        X = sb("X", [P, NP, P])
        M = sb("M", [P, NP, P])
        GQ2 = sb("GQ", [P, 2, NP, T])
        W = sb("W", [P, NP, T])
        Z = sb("Z", [P, NP, T])
        ZS = Z[:, 0:2, :].rearrange("p a (b n) -> p (a b) n", n=32)
        T12 = sb("T1", [P, 2, NP, T])
        DQ = sb("DQ", [P, NP, T])
        OT = sb("OT", [P, 2, GT])
        CT = sb("CT", [CD, GT])
        VT = sb("VT", [P, 8, CD])
        VB = sb("VB", [P, 64, 2, 9])
        MX = sb("MX", [P, 4, 8])
        RS = sb("RS", [P, 32])
        OB = W[:, :, :].rearrange("p a t -> p (a t)").rearrange("p (n d) -> p n d", d=D8)
        SMALL = sb("SMALL", [P, 8])
        ONES = sb("ONES", [P, 1])
        ZW = sb("ZW", [P, P], F16)

        EA = SCR[:, 0:4096].rearrange("p (h a t) -> p h a t", h=NH, a=NP)
        EQ = SCR[:, 4096:8192].rearrange("p (h a t) -> p h a t", h=NH, a=NP)
        KG = SCR[:, 0:4096].rearrange("p (c b g t) -> p c b g t", c=2, b=8, g=4)
        ES = SCR[:, 4096:6144].rearrange("p (c r g t) -> p c r g t", c=2, r=4, g=4)
        PT = SCR[:, 6144:8192].rearrange("p (r q s) -> p r q s", r=4, q=4)
        H = SCR[:, 0:4096].rearrange("p (f t) -> p f t", f=FB)
        HH = SCR[:, 4096:6144].bitcast(F16).rearrange("p (f t) -> p f t", f=FB)
        HL = SCR[:, 6144:8192].bitcast(F16).rearrange("p (f t) -> p f t", f=FB)
        QT = KQ
        RHA = Y[:, 0:2, :].rearrange("p a (b t) -> p (a b) t", t=T)
        RHQ = Y[:, 2:4, :].rearrange("p a (b t) -> p (a b) t", t=T)

        ident = CST[:, C_ID:C_ID + 128]
        identc = CST[:, C_IC:C_IC + 64]

        def mt(k):
            return CST[:, C_MT + 64 * k:C_MT + 64 * k + 64]

        def over_pairs(m, n=NP):
            return m[:, None, :].broadcast_to([P, n, T])

        PJ = [ctx.enter_context(nc.psum_tensor(f"PJ{i}", [P, GT], F32)) for i in range(2)]
        CA, CB, BA, BB = [ctx.enter_context(nc.psum_tensor(n, [P, GT], F32)) for n in ("CA", "CB", "BA", "BB")]
        AC = [ctx.enter_context(nc.psum_tensor(f"AC{i}", [P, GT], F32)) for i in range(2)]
        gram = PJ[0][:, :].rearrange("p (a k t) -> p a k t", a=NP, k=2)
        psR = PJ[1][:, 0:256].rearrange("p (a t) -> p a t", a=NP)
        psS = PJ[1][:, 256:256 + 2 * NP]
        psM = BB[:, 0:256].rearrange("p (a t) -> p a t", a=NP)
        psW = [b[:, 0:128].rearrange("p (a t) -> p a t", a=2) for b in (CA, CB)]
        psP = [b[:, 128:256].rearrange("p (a t) -> p a t", a=2) for b in (CA, CB)]
        psX = [b[:, 0:256].rearrange("p (a t) -> p a t", a=2) for b in (BA, BB)]

        def chain(c):
            return slice(2 * c, 2 * c + 2)

        names = """ld_const ld_w0 ld_w1 ld_w2 ld_w3
            w_split w_hi tern_sum tern_all tern_done zeroed conv_scaled""".split()
        owned = {
            "sync": "ld_x ld_ctx st_out",
            "pool": "x_copied rhq_done masked rsq sq rstd vb_done",
            "act": "xh_done gate_s dec_exp tap kq x_bd ot_done v_done exp_done pt_done gelu_done",
            "dve": """ln_step xl_done gate_v rha_done cw_cur conv scale_done dq_done a_done gq_done t1_done w_done_v z_done m_done
                      x1_done kg_done mx_done sub_done rs_done ob_done nrm_done hh_done hl_done y_done x3_done""",
            "pe": """tr_done gate_mm dec_mm proj gram_mm ss_mm r_mm w_mm t_mm p_mm m_mm o_mm vt_mm op_mm
                     rep_mm sc_mm pt_mm pv_mm f1_mm f2_mm""",
        }
        names += " ".join(owned.values()).split()
        S = {n: sem(n) for n in names}
        LW = [S[f"ld_w{n}"] for n in range(4)]

        def start_counts(eng, who):
            for n in owned[who].split():
                eng.sem_inc(S[n], 1)

        def at(count):
            return count + 1

        block = ctx.enter_context(nc.Block())

        @block.sync
        def _(sp):
            start_counts(sp, "sync")
            sp.dma_start(CST[:, :], cst).then_inc(S["ld_const"], 16)
            sp.dma_start(CW[:, :, :], cw).then_inc(S["ld_const"], 16)
            sp.dma_start(AB32[:, :, :], wab).then_inc(S["ld_const"], 16)
            sp.dma_start(B1[:, :], b1).then_inc(S["ld_const"], 16)
            sp.dma_start(B2[:, :], b2).then_inc(S["ld_const"], 16)
            sp.dma_start(XP[:, :, :], x[0]).then_inc(S["ld_x"], 16)
            for n in range(8):
                if n >= 4:
                    sp.wait_ge(S["w_split"], n - 3)
                sp.dma_start(SCR[:, (n % 4) * 2048:(n % 4 + 1) * 2048],
                             wall[n // 4][:, (n % 4) * 2048:(n % 4 + 1) * 2048]).then_inc(LW[n % 4], 16)
            sp.dma_start(WO[:, :, :], wo).then_inc(S["ld_const"], 16)
            sp.wait_ge(S["w_split"], 6)
            sp.dma_start(SCR[:, 0:2048], w1).then_inc(LW[0], 16)
            sp.dma_start(SCR[:, 2048:4096], w2).then_inc(LW[1], 16)

            def group(g, last):
                sp.wait_ge(S["kg_done"], at(g * 2))
                sp.wait_ge(S["vb_done"], at(g * 2))
                one = ds(g, 1)
                sp.dma_start(CT[:, :], ctxT[one].rearrange("a c t -> (a c) t")).then_inc(S["ld_ctx"], 16)
                sp.dma_start(VT[0:64, :, :], ctxR[one].rearrange("a t b c -> (a t) b c")).then_inc(S["ld_ctx"], 16)
                sp.dma_start(VT[64:128, :, :], ctxR[one].rearrange("a t b c -> (a t) b c")).then_inc(S["ld_ctx"], 16)
                if not last:
                    sp.wait_ge(S["x_copied"], at(g + 1))
                    sp.wait_ge(S["ln_step"], at(g * 39 + 13))
                    sp.dma_start(XP[:, :, :], x[ds(g + 1, 1)].rearrange("a p n e -> (a p) n e")).then_inc(S["ld_x"], 16)
                sp.wait_ge(S["x3_done"], at(g * 2 + 2))
                sp.dma_start(out[one].rearrange("a p n e -> (a p) n e"), XC[:, :, :]).then_inc(S["st_out"], 16)

            with sp.Fori(0, G - 1) as g:
                group(g, False)
            group(G - 1, True)
            sp.wait_ge(S["st_out"], at(16 * G))

        @block.gpsimd
        def _(pool):
            start_counts(pool, "pool")
            pool.wait_ge(S["tern_sum"], 2)
            nc.gpsimd.partition_all_reduce(SMALL[:, 2:4], SMALL[:, 0:2], P, bass.bass_isa.ReduceOp.add).then_inc(S["tern_all"], 1)
            nc.gpsimd.memset(VB[:, :, :, :], 0.0).then_inc(S["zeroed"], 1)
            pool.wait_ge(S["zeroed"], 1)
            nc.gpsimd.memset(VB[:, :, :, 8:9], 0.0).then_inc(S["zeroed"], 1)
            pool.wait_ge(S["zeroed"], 2)
            nc.gpsimd.memset(VB[0:64, :, 0, 8:9], 1.0).then_inc(S["zeroed"], 1)
            pool.wait_ge(S["zeroed"], 3)
            nc.gpsimd.memset(VB[64:128, :, 1, 8:9], 1.0).then_inc(S["zeroed"], 1)
            pool.wait_ge(S["zeroed"], 4)
            nc.gpsimd.memset(MHALF[:, :], -0.5).then_inc(S["zeroed"], 1)
            pool.wait_ge(S["zeroed"], 5)
            pool.wait_ge(S["ld_const"], 96)

            def rstd(nid):
                pool.wait_ge(S["ln_step"], at(nid * 13 + 9))
                nc.gpsimd.tensor_tensor(RSTD[:, :], VE[:, :], MHALF[:, 0:NP], ALU.pow).then_inc(S["rstd"], 1)

            def inverse_norms(it):
                pool.wait_ge(S["scale_done"], at(it * 4 + 1))
                nc.gpsimd.tensor_tensor(NQ[:, :, :].rearrange("p k a -> p (k a)"), SSM[:, :], MHALF[:, :], ALU.pow).then_inc(S["rsq"], 1)

            def masked(it, h):
                pool.wait_ge(S["scale_done"], at(it * 4))
                nc.gpsimd.tensor_tensor(EAM[:, :, :], EA[:, ds(h, 1), :, :].rearrange("p o a t -> p (o a) t"),
                                        over_pairs(CST[:, C_MA:C_MA + 64]), ALU.mult).then_inc(S["masked"], 1)
                pool.wait_ge(S["gq_done"], at(it))
                nc.gpsimd.tensor_tensor(EQM[:, :, :], EQ[:, ds(h, 1), :, :].rearrange("p o a t -> p (o a) t"),
                                        over_pairs(CST[:, C_MQ:C_MQ + 64]), ALU.mult).then_inc(S["masked"], 1)

            def squares(it):
                pool.wait_ge(S["ss_mm"], at(it))
                for n, a in enumerate((1, 0)):
                    pool.wait_ge(S["kq"], at(it * 2 + n + 1))
                    nc.gpsimd.tensor_tensor(SQ[:, a, :], KQ[:, a, :], KQ[:, a, :], ALU.mult).then_inc(S["sq"], 1)

            with pool.Fori(0, G) as g:
                pool.wait_ge(S["ld_x"], at(g * 16 + 16))
                pool.wait_ge(S["st_out"], at(g * 16))
                pool.nop(nofuse=True)
                nc.gpsimd.tensor_copy(XC[:, :, :], XP[:, :, :]).then_inc(S["x_copied"], 1)
                rstd(g * 3)
                pool.wait_ge(S["gate_v"], at(g * 6 + 6))
                for p in range(NP):
                    if p:
                        pool.wait_ge(S["dec_mm"], at(g * 16 + 4 * p))
                    nc.gpsimd.tensor_tensor(RHQ, CST[:, C_UTC:C_UTC + 64][:, None, :].broadcast_to([P, NH, T]),
                                            LA[:, p, :][:, :, None].broadcast_to([P, NH, T]), ALU.mult).then_inc(S["rhq_done"], 1)
                pool.wait_ge(S["dec_exp"], at(g * 16 + 16))
                masked(g * NH, 0)
                squares(g * NH)
                inverse_norms(g * NH)
                with pool.Fori(1, NH) as h:
                    masked(g * NH + h, h)
                    squares(g * NH + h)
                    inverse_norms(g * NH + h)
                rstd(g * 3 + 1)
                pool.wait_ge(S["ld_ctx"], at(g * 48 + 48))
                pool.wait_ge(S["pv_mm"], at(g * 4))
                pool.nop(nofuse=True)
                for n in range(2):
                    pool.wait_ge(S["vb_done"], at(g * 2 + n))
                    pool.nop(nofuse=True)
                    nc.gpsimd.tensor_copy(VB[64 * n:64 * n + 64, :, n, 0:8],
                                          VT[64 * n:64 * n + 64, :, :].rearrange("p b (k d) -> p (b k) d", d=D8)).then_inc(S["vb_done"], 1)
                pool.wait_ge(S["vb_done"], at(g * 2 + 2))
                rstd(g * 3 + 2)

        @block.scalar
        def _(act):
            start_counts(act, "act")
            for n in range(8):
                act.wait_ge(LW[n % 4], 16 * (n // 4 + 1))
                nc.scalar.activation(WH[:, n // 4, (n % 4) * 2048:(n % 4 + 1) * 2048], SCR[:, (n % 4) * 2048:(n % 4 + 1) * 2048],
                                     ACT.Copy, scale=WS).then_inc(S["w_hi"], 1)

            def transposed(nid, n):
                for c in range(2):
                    act.wait_ge(S["tr_done"], at(nid * 2 + c + 1))
                    if n == 1:
                        nc.scalar.activation(QT[:, c, :], PJ[c][:, :], ACT.Copy).then_inc(S["xh_done"], 1)
                    else:
                        nc.scalar.activation(XH[:, c, 0:GT], PJ[c][:, :], ACT.Copy).then_inc(S["xh_done"], 1)

            def tap(it, b):
                act.wait_ge(S["proj"], at(it * 4 + b + 1))
                act.wait_ge(S["cw_cur"], at(it + 1))
                act.wait_ge(S["vt_mm"], at(it * 2))
                act.wait_ge(S["kq"], at(it * 2))
                nc.scalar.activation(Y[:, b, :], PJ[b % 2][:, :], ACT.Identity, scale=CWC[:, 5 * b + 3:5 * b + 4],
                                     bias=CWC[:, 5 * b + 4:5 * b + 5]).then_inc(S["tap"], 1)

            def silu_kq(it, b):
                act.wait_ge(S["conv"], at(it * 12 + 3 * b + 3))
                act.wait_ge(S["gram_mm"], at(it))
                act.wait_ge(S["sq"], at(it * 2))
                nc.scalar.activation(KQ[:, 1 - b, :], Y[:, b, :], ACT.Silu).then_inc(S["kq"], 1)

            def silu_v(it, b):
                act.wait_ge(S["vt_mm"], at(it * 2 + b - 1))
                act.wait_ge(S["o_mm"], at(it * 2))
                nc.scalar.activation(V[:, :, (b - 2) * P:(b - 1) * P], (BA, BB)[b - 2][:, :].rearrange("p (a n) -> p a n", a=NP),
                                     ACT.Silu).then_inc(S["v_done"], 1)

            def x_diag(it, k, c):
                act.wait_ge(S["t_mm"], at(it * 12 + 2 * (k - 1) + c + 1))
                if k == 1:
                    act.wait_ge(S["m_mm"], at(it))
                else:
                    act.wait_ge(S["p_mm"], at(it * 10 + 2 * (k - 2) + c + 1))
                for n in range(2):
                    lo = 64 * n
                    nc.scalar.activation(X[lo:lo + 64, chain(c), lo:lo + 64], psX[c][0:64, :, lo:lo + 64], ACT.Copy).then_inc(S["x_bd"], 1)

            def o_out(it):
                for n, src in enumerate(PJ):
                    act.wait_ge(S["o_mm"], at(it * 2 + n + 1))
                    act.wait_ge(S["op_mm"], at(it))
                    nc.scalar.activation(OT[:, n, :], src[:, :], ACT.Copy).then_inc(S["ot_done"], 1)

            act.wait_ge(S["ld_const"], 96)
            with act.Fori(0, G) as g:
                transposed(g * 3, 0)
                act.wait_ge(S["gate_v"], at(g * 6 + 3))
                nc.scalar.activation(LT[:, 2], LT[:, 0], ACT.Exp, scale=-1.0).then_inc(S["gate_s"], 1)
                nc.scalar.activation(LT[:, 3], ZS[:, :, 16:32], ACT.Exp, scale=-1.0).then_inc(S["gate_s"], 1)
                act.wait_ge(S["gate_v"], at(g * 6 + 4))
                act.wait_ge(S["gate_s"], at(g * 3 + 1))
                nc.scalar.activation(LT[:, 0], LT[:, 2], ACT.Ln).then_inc(S["gate_s"], 1)
                for p in range(NP):
                    for n, src in enumerate((CA, CB, BA, BB)):
                        act.wait_ge(S["dec_mm"], at(g * 16 + 4 * p + n + 1))
                        act.wait_ge(S["x3_done"], at(g * 2))
                        dst = (EA if n < 2 else EQ)[:, (n % 2) * 8:(n % 2) * 8 + 8, p, :]
                        nc.scalar.activation(dst, src[:, :].rearrange("p (h t) -> p h t", h=8), ACT.Exp).then_inc(S["dec_exp"], 1)
                it0 = g * NH
                tap(it0, 0)
                tap(it0, 1)
                silu_kq(it0, 0)
                tap(it0, 2)
                silu_kq(it0, 1)
                tap(it0, 3)
                silu_v(it0, 2)
                silu_v(it0, 3)

                def head(j, i):
                    if i is not None:
                        tap(i, 0)
                    for k in range(1, LV + 1):
                        x_diag(j, k, 0)
                        x_diag(j, k, 1)
                        if i is not None:
                            if k <= 3:
                                tap(i, k)
                            if k <= 2:
                                silu_kq(i, k - 1)
                    o_out(j)
                    if i is not None:
                        silu_v(i, 2)
                        silu_v(i, 3)

                head(it0, it0 + 1)
                with act.Fori(1, NH - 1) as h:
                    head(g * NH + h, g * NH + h + 1)
                head(g * NH + NH - 1, None)

                transposed(g * 3 + 1, 1)
                for p in range(NP):
                    pid = g * NP + p
                    for r in range(4):
                        act.wait_ge(S["sub_done"], at(pid * 4 + r + 1))
                        nc.scalar.activation(ES[:, :, r], ES[:, :, r], ACT.Exp, scale=float(D8) ** -0.5).then_inc(S["exp_done"], 1)
                    for r in range(4):
                        act.wait_ge(S["pt_mm"], at(pid * 4 + r + 1))
                        act.wait_ge(S["pv_mm"], at(pid))
                        nc.scalar.activation(PT[:, r], PJ[r % 2][:, :].rearrange("p (q s) -> p q s", q=4), ACT.Copy).then_inc(S["pt_done"], 1)
                transposed(g * 3 + 2, 2)
                for f in range(FB):
                    act.wait_ge(S["f1_mm"], at(g * FB + f + 1))
                    nc.scalar.activation(H[:, f, :], (CA, CB, BA, BB)[f % 4][:, :], ACT.Gelu, bias=B1[:, f:f + 1]).then_inc(S["gelu_done"], 1)

        @block.vector
        def _(dve):
            start_counts(dve, "dve")
            V_ = nc.vector
            for n in range(8):
                dve.wait_ge(S["w_hi"], n + 1)
                sl = slice((n % 4) * 2048, (n % 4 + 1) * 2048)
                V_.scalar_tensor_tensor(WL[:, n // 4, sl], SCR[:, sl], WS, WH[:, n // 4, sl], ALU.mult, ALU.subtract).then_inc(S["w_split"], 1)
            dve.wait_ge(S["ld_const"], 96)
            V_.tensor_copy(ABH[:, :, :], AB32[:, :, :]).then_inc(S["conv_scaled"], 1)
            cwv = CW[:, :, :].rearrange("p h (b n) -> p (h b) n", n=5)[:, :, 0:4]
            V_.tensor_scalar(cwv, cwv, 1.0 / WS, None, ALU.mult).then_inc(S["conv_scaled"], 1)
            dve.wait_ge(S["conv_scaled"], 2)
            V_.tensor_tensor(ABL[:, :, :], AB32[:, :, :], ABH[:, :, :], ALU.subtract).then_inc(S["conv_scaled"], 1)
            for m in (A, X, M):
                V_.memset(m[:, :, :], 0.0).then_inc(S["conv_scaled"], 1)
            V_.memset(ONES[:, :], 1.0).then_inc(S["conv_scaled"], 1)
            V_.memset(ZW[:, :], 0.0).then_inc(S["conv_scaled"], 1)
            V_.memset(XH[:, :, GT:GT + 1], 0.0).then_inc(S["conv_scaled"], 1)
            V_.memset(XL[:, :, GT:GT + 1], 0.0).then_inc(S["conv_scaled"], 1)
            dve.wait_ge(LW[0], 48)
            dve.wait_ge(LW[1], 48)
            for n in range(2):
                V_.tensor_reduce(SMALL[:, n:n + 1], SCR[:, 2048 * n:2048 * n + 2048], AX_X, ALU.add,
                                 apply_absolute_value=True).then_inc(S["tern_sum"], 1)
            dve.wait_ge(S["tern_all"], 1)
            V_.tensor_scalar(SMALL[:, 4:6], SMALL[:, 2:4], 1.0 / (E * F), 1e-8, ALU.mult, ALU.max).then_inc(S["tern_done"], 1)
            dve.wait_ge(S["tern_done"], 1)
            V_.tensor_scalar(SMALL[:, 6:8], SMALL[:, 4:6], -0.5, None, ALU.mult).then_inc(S["tern_done"], 1)
            V_.tensor_scalar(SMALL[:, 0:2], SMALL[:, 4:6], 0.5, None, ALU.mult).then_inc(S["tern_done"], 1)
            dve.wait_ge(S["tern_done"], 3)
            for n, dst in enumerate((W1[:, :, :].rearrange("p c f -> p (c f)"), W2[:, :, :].rearrange("p f e -> p (f e)"))):
                w = SCR[:, 2048 * n:2048 * n + 2048]
                V_.tensor_scalar(SCR[:, 4096 + 2048 * n:6144 + 2048 * n], w, SMALL[:, 6 + n:7 + n], None, ALU.is_lt).then_inc(S["tern_done"], 1)
                dve.wait_ge(S["tern_done"], 4 + 2 * n)
                V_.scalar_tensor_tensor(dst, w, SMALL[:, n:n + 1], SCR[:, 4096 + 2048 * n:6144 + 2048 * n], ALU.is_gt, ALU.subtract).then_inc(S["tern_done"], 1)

            def norm(nid, src):
                dve.wait_ge(S["ln_step"], at(nid * 13))
                for p in range(NP):
                    V_.bn_stats(STT6[:, p, :], src[:, p, :]).then_inc(S["ln_step"], 1)
                dve.wait_ge(S["ln_step"], at(nid * 13 + 4))
                dve.nop(nofuse=True)
                for p in range(NP):
                    V_.bn_aggr(MV[:, p, :], STT6[:, p, :]).then_inc(S["ln_step"], 1)
                dve.wait_ge(S["ln_step"], at(nid * 13 + 8))
                V_.tensor_scalar(VE[:, :], MV[:, :, 1], 1e-5, None, ALU.add).then_inc(S["ln_step"], 1)
                dve.wait_ge(S["rstd"], at(nid + 1))
                dve.wait_ge(S["tr_done"], at(nid * 2))
                for p in range(NP):
                    V_.tensor_scalar(XN[:, p, :], src[:, p, :], MV[:, p, 0:1], RSTD[:, p:p + 1], ALU.subtract, ALU.mult).then_inc(S["ln_step"], 1)

            def low_parts(nid, lid):
                for c in range(2):
                    dve.wait_ge(S["xh_done"], at(nid * 2 + c + 1))
                    V_.tensor_tensor(XL[:, c, 0:GT], PJ[c][:, :], XH[:, c, 0:GT], ALU.subtract).then_inc(S["xl_done"], 1)

            def cw_cur(it, h):
                dve.wait_ge(S["tap"], at(it * 4))
                dve.wait_ge(S["conv"], at(it * 12))
                V_.tensor_copy(CWC[:, :], CW[:, ds(h, 1), :].rearrange("p o n -> p (o n)")).then_inc(S["cw_cur"], 1)
                dve.wait_ge(S["cw_cur"], at(it + 1))

            def conv(it, b, m):
                if m == 1:
                    dve.wait_ge(S["tap"], at(it * 4 + b + 1))
                else:
                    dve.wait_ge(S["conv"], at(it * 12 + 3 * b + m - 1))
                yv = Y[:, b, :].rearrange("p (n t) -> p n t", t=T)
                pv = PJ[b % 2][:, :].rearrange("p (n t) -> p n t", t=T)
                V_.scalar_tensor_tensor(yv[:, :, m:T], pv[:, :, 0:T - m], CWC[:, 5 * b + 3 - m:5 * b + 4 - m], yv[:, :, m:T],
                                        ALU.mult, ALU.add).then_inc(S["conv"], 1)

            def squared_norms(j):
                dve.wait_ge(S["ss_mm"], at(j + 1))
                V_.tensor_scalar(SSM[:, :], psS, 1e-24, None, ALU.max).then_inc(S["scale_done"], 1)

            def scales(j, h):
                dve.wait_ge(S["rsq"], at(j + 1))
                dve.wait_ge(S["t1_done"], at(j))
                V_.tensor_tensor(NBT[:, :], NQ[:, 0, :], BE[:, ds(h, 1), :].rearrange("p o a -> p (o a)"), ALU.mult).then_inc(S["scale_done"], 1)
                dve.wait_ge(S["r_mm"], at(j))
                V_.tensor_tensor(DQ[:, :, :], over_pairs(identc), NQ[:, 1, :][:, :, None].broadcast_to([P, NP, T]), ALU.mult).then_inc(S["dq_done"], 1)
                dve.wait_ge(S["scale_done"], at(j * 4 + 2))
                V_.tensor_tensor(RA[:, :], NBT[:, :], NQ[:, 0, :], ALU.mult).then_inc(S["scale_done"], 1)
                dve.wait_ge(S["scale_done"], at(j * 4 + 3))
                dve.wait_ge(S["masked"], at(j * 2 + 2))
                dve.wait_ge(S["a_done"], at(j * 2))
                V_.tensor_tensor(EAR[:, :, :], EAM[:, :, :], RA[:, :][:, :, None].broadcast_to([P, NP, T]), ALU.mult).then_inc(S["scale_done"], 1)

            def a_diag(j):
                dve.wait_ge(S["scale_done"], at(j * 4 + 4))
                dve.wait_ge(S["gram_mm"], at(j + 1))
                dve.wait_ge(S["w_mm"], at(j * 12))
                for n in range(2):
                    lo = 64 * n
                    V_.tensor_tensor(A[lo:lo + 64, :, lo:lo + 64], gram[lo:lo + 64, :, 0, :], EAR[lo:lo + 64, :, :], ALU.mult).then_inc(S["a_done"], 1)

            def query_side(j, par):
                V_.tensor_tensor(GQ2[:, par], gram[:, :, 1, :], EQM[:, :, :], ALU.mult).then_inc(S["gq_done"], 1)
                dve.wait_ge(S["r_mm"], at(j + 1))
                V_.tensor_tensor(T12[:, par], psR, NBT[:, :][:, :, None].broadcast_to([P, NP, T]), ALU.mult).then_inc(S["t1_done"], 1)

            def w_masked(j, k, c):
                dve.wait_ge(S["w_mm"], at(j * 12 + 2 * k + c + 1))
                if k == 0:
                    dve.wait_ge(S["p_mm"], at(j * 10))
                V_.tensor_tensor(W[:, chain(c), :], psW[c], over_pairs(mt(k), 2), ALU.mult).then_inc(S["w_done_v"], 1)

            def z_next(j, k, c):
                zc = Z[:, chain(c), :]
                if k == 0:
                    dve.wait_ge(S["w_done_v"], at(j * 12 + c + 1))
                    dve.wait_ge(S["t_mm"], at(j * 12))
                    V_.tensor_tensor(zc, over_pairs(identc, 2), W[:, chain(c), :], ALU.subtract).then_inc(S["z_done"], 1)
                else:
                    dve.wait_ge(S["z_done"], at(j * 12 + 2 * (k - 1) + c + 1))
                    dve.wait_ge(S["p_mm"], at(j * 10 + 2 * (k - 1) + c + 1))
                    V_.tensor_tensor(zc, zc, psP[c], ALU.subtract).then_inc(S["z_done"], 1)

            def m_diag(j, par):
                dve.wait_ge(S["m_mm"], at(j + 1))
                dve.wait_ge(S["t1_done"], at(j + 1))
                dve.wait_ge(S["o_mm"], at(j * 2))
                for c in range(2):
                    for n in range(2):
                        lo = 64 * n
                        V_.tensor_tensor(M[lo:lo + 64, chain(c), lo:lo + 64], psM[lo:lo + 64, chain(c)], T12[lo:lo + 64, par, chain(c), :],
                                         ALU.mult).then_inc(S["m_done"], 1)

            with dve.Fori(0, G) as g:
                dve.wait_ge(S["ld_x"], at(g * 16 + 16))
                norm(g * 3, XP)
                low_parts(g * 3, 0)
                dve.wait_ge(S["gate_mm"], at(g + 1))
                dve.wait_ge(S["gate_v"], at(g * 6))
                V_.tensor_copy(ZS[:, :, :], BB[:, 0:128].rearrange("p (a n) -> p a n", a=NP)).then_inc(S["gate_v"], 1)
                dve.wait_ge(S["gate_v"], at(g * 6 + 1))
                V_.scalar_tensor_tensor(LT[:, 0], ZS[:, :, 0:16], -1.0, ZS[:, :, 0:16], ALU.mult, ALU.max).then_inc(S["gate_v"], 1)
                V_.tensor_scalar(LT[:, 1], ZS[:, :, 0:16], 0.0, None, ALU.min).then_inc(S["gate_v"], 1)
                dve.wait_ge(S["gate_s"], at(g * 3 + 2))
                V_.tensor_scalar(LT[:, 2:4], LT[:, 2:4], 1.0, None, ALU.add).then_inc(S["gate_v"], 1)
                dve.wait_ge(S["gate_v"], at(g * 6 + 4))
                V_.reciprocal(BE[:, :, :].rearrange("p h a -> p a h"), LT[:, 3]).then_inc(S["gate_v"], 1)
                dve.wait_ge(S["gate_s"], at(g * 3 + 3))
                dve.wait_ge(S["rha_done"], at(g * NP))
                V_.tensor_tensor(LA[:, :, :], LT[:, 1], LT[:, 0], ALU.subtract).then_inc(S["gate_v"], 1)
                dve.wait_ge(S["gate_v"], at(g * 6 + 6))
                for p in range(NP):
                    if p:
                        dve.wait_ge(S["dec_mm"], at(g * 16 + 4 * p - 2))
                    V_.tensor_tensor(RHA, CST[:, C_LEC:C_LEC + 64][:, None, :].broadcast_to([P, NH, T]),
                                     LA[:, p, :][:, :, None].broadcast_to([P, NH, T]), ALU.mult).then_inc(S["rha_done"], 1)

                it0 = g * NH
                cw_cur(it0, 0)
                for b in range(4):
                    for m in (1, 2, 3):
                        conv(it0, b, m)

                squared_norms(it0)
                scales(it0, 0)
                a_diag(it0)
                query_side(it0, 0)

                after_w = [[], [(0, 2), (0, 3)], [(1, 2), (1, 3)], [(2, 2), (2, 3)], [(3, 2), (3, 3)], []]
                after_z = [[(0, 1)], [(1, 1)], [(2, 1)], [(3, 1)], [], []]

                def head(j, par, i, hi):
                    if i is not None:
                        cw_cur(i, hi)
                    for k in range(LV):
                        for c in range(2):
                            w_masked(j, k, c)
                        if i is not None:
                            for b, m in after_w[k]:
                                conv(i, b, m)
                        for c in range(2):
                            z_next(j, k, c)
                        if i is not None:
                            for b, m in after_z[k]:
                                conv(i, b, m)
                            if k == 4:
                                squared_norms(i)
                            if k == 5:
                                scales(i, hi)
                                a_diag(i)
                                query_side(i, 1 - par)
                    m_diag(j, par)

                head(it0, 0, it0 + 1, 1)
                with dve.Fori(0, NH // 2 - 1) as h2:
                    for odd in range(2):
                        h = h2 * 2 + 1 + odd
                        head(g * NH + h, 1 - odd, g * NH + h + 1, h + 1)
                head(g * NH + NH - 1, 1, None, None)

                dve.wait_ge(S["op_mm"], at(g * NH + NH))
                dve.wait_ge(S["x_copied"], at(g + 1))
                for n in range(2):
                    xv = XC[:, 2 * n:2 * n + 2, :].rearrange("p a e -> p (a e)")
                    V_.tensor_tensor(xv, AC[n][:, :], xv, ALU.add).then_inc(S["x1_done"], 1)
                dve.wait_ge(S["x1_done"], at(g * 2 + 2))
                norm(g * 3 + 1, XC)
                for c, src in enumerate((CA, CB)):
                    dve.wait_ge(S["rep_mm"], at(g * 2 + c + 1))
                    for b in range(8):
                        ins = V_.tensor_tensor(KG[:, c, b], src[:, T * b:T * b + T][:, None, :].broadcast_to([P, 4, T]),
                                               CST[:, C_GM:C_GM + 4][:, :, None].broadcast_to([P, 4, T]), ALU.mult)
                    ins.then_inc(S["kg_done"], 1)

                def softmax_in(p):
                    pid = g * NP + p
                    for r, src in enumerate((CA, CB, BA, BB)):
                        sv = src[:, :].rearrange("p (c g t) -> p c g t", c=2, g=4)
                        dve.wait_ge(S["sc_mm"], at(pid * 4 + r + 1))
                        dve.wait_ge(S["sub_done"], at(pid * 4 + r))
                        V_.tensor_reduce(MX[:, r, :], src[:, :].rearrange("p (n t) -> p n t", t=T), AX_X, ALU.max).then_inc(S["mx_done"], 1)
                        dve.wait_ge(S["mx_done"], at(pid * 4 + r + 1))
                        if r == 0:
                            dve.wait_ge(S["pt_mm"], at(pid * 4))
                        V_.tensor_tensor(ES[:, :, r], sv, MX[:, r, :].rearrange("p (c g) -> p c g", c=2)[:, :, :, None].broadcast_to([P, 2, 4, T]),
                                         ALU.subtract).then_inc(S["sub_done"], 1)

                def softmax_out(p):
                    pid = g * NP + p
                    pv = AC[p % 2][:, 0:288].rearrange("p (n d) -> p n d", d=9)
                    dve.wait_ge(S["pv_mm"], at(pid + 1))
                    dve.wait_ge(S["ob_done"], at(pid))
                    V_.reciprocal(RS[:, :], pv[:, :, 8]).then_inc(S["rs_done"], 1)
                    dve.wait_ge(S["rs_done"], at(pid + 1))
                    dve.wait_ge(S["nrm_done"], at(pid))
                    V_.tensor_tensor(OB[:, :, :], pv[:, :, 0:8], RS[:, :][:, :, None].broadcast_to([P, 32, D8]), ALU.mult).then_inc(S["ob_done"], 1)
                    dve.wait_ge(S["ob_done"], at(pid + 1))
                    V_.tensor_tensor(XC[:, p, :], XC[:, p, :], OB[:, :, :].rearrange("p n d -> p (n d)"), ALU.add).then_inc(S["nrm_done"], 1)

                for p in range(NP):
                    softmax_in(p)
                    if p:
                        softmax_out(p - 1)
                softmax_out(NP - 1)
                dve.wait_ge(S["nrm_done"], at(g * NP + NP))
                norm(g * 3 + 2, XC)
                low_parts(g * 3 + 2, 1)
                for f in range(FB):
                    dve.wait_ge(S["gelu_done"], at(g * FB + f + 1))
                    V_.tensor_copy(HH[:, f, :], H[:, f, :]).then_inc(S["hh_done"], 1)
                    dve.wait_ge(S["hh_done"], at(g * FB + f + 1))
                    V_.tensor_tensor(HL[:, f, :], H[:, f, :], HH[:, f, :], ALU.subtract).then_inc(S["hl_done"], 1)
                dve.wait_ge(S["f2_mm"], at(g + 1))
                for n in range(2):
                    xv = XC[:, 2 * n:2 * n + 2, :]
                    V_.tensor_tensor(xv, AC[n][:, :].rearrange("p (a e) -> p a e", a=2), xv, ALU.add).then_inc(S["y_done"], 1)
                dve.wait_ge(S["y_done"], at(g * 2 + 2))
                for n in range(2):
                    xv = XC[:, 2 * n:2 * n + 2, :]
                    V_.tensor_tensor(xv, xv, B2[:, :][:, None, :].broadcast_to([P, 2, E]), ALU.add).then_inc(S["x3_done"], 1)

        @block.tensor
        def _(pe):
            start_counts(pe, "pe")
            mm = nc.tensor.matmul
            pe.wait_ge(S["ld_const"], 96)
            pe.wait_ge(S["conv_scaled"], 10)
            pe.wait_ge(S["tern_done"], 7)
            pe.wait_ge(S["zeroed"], 4)
            pe.wait_ge(S["w_hi"], 8)

            def transposes(nid):
                pe.wait_ge(S["ln_step"], at(nid * 13 + 13))
                for c in range(2):
                    for p in range(NP):
                        ins = nc.tensor.transpose(PJ[c][:, P * p:P * p + P], XN[:, p, P * c:P * c + P], ident)
                    ins.then_inc(S["tr_done"], 1)

            TERMS = [(WH, XH), (WH, XL), (WL, XH)]

            def project(it, h, b, drained=None, inner=False):
                if b >= 2:
                    pe.wait_ge(S["conv"], at(it * 12 + 3 * b - 3))
                else:
                    pe.wait_ge(S["ot_done"], at(drained + b if inner else drained))
                    pe.wait_ge(S["gq_done"], at(it))
                    pe.wait_ge(S["t1_done"], at(it))
                n = 0
                for c in range(2):
                    for wt, xt in TERMS:
                        ins = mm(PJ[b % 2][:, :], wt[:, c, ds(h * 512 + b * P, P)], xt[:, c, 0:GT], start=(n == 0), stop=(n == 5))
                        n += 1
                ins.then_inc(S["proj"], 1)

            def grams(j):
                pe.wait_ge(S["kq"], at(j * 2 + 2))
                pe.wait_ge(S["conv"], at(j * 12 + 9))
                for p in range(NP):
                    for n in range(2):
                        c0 = P * p + 64 * n
                        ins = mm(gram[64 * n:64 * n + 64, p], KQ[:, 0, c0:c0 + 64], KQ[:, :, c0:c0 + 64], start=True, stop=True)
                ins.then_inc(S["gram_mm"], 1)

            def norms(j):
                pe.wait_ge(S["sq"], at(j * 2 + 2))
                pe.wait_ge(S["conv"], at(j * 12 + 12))
                for a in range(2):
                    for p in range(NP):
                        ins = mm(psS[:, a * NP + p:a * NP + p + 1], SQ[:, a, P * p:P * p + P], ONES[:, :], start=True, stop=True)
                ins.then_inc(S["ss_mm"], 1)

            def spread_q(j):
                pe.wait_ge(S["dq_done"], at(j + 1))
                mm(PJ[1][:, 0:256], CST[:, C_ON:C_ON + 128], DQ[:, :, :].rearrange("p a t -> p (a t)"), start=True, stop=True).then_inc(S["r_mm"], 1)

            def w_level(j, k, c):
                if k == 0:
                    pe.wait_ge(S["a_done"], at(j * 2 + 2))
                else:
                    pe.wait_ge(S["z_done"], at(j * 12 + 2 * (k - 1) + c + 1))
                if k == 1:
                    pe.wait_ge(S["v_done"], at(j * 2 + 2))
                for a in (2 * c, 2 * c + 1):
                    ins = mm(psW[c][:, a % 2], A[:, a, :], identc if k == 0 else Z[:, a, :], start=True, stop=True)
                ins.then_inc(S["w_mm"], 1)

            def t_level(j, k, c):
                if k == LV:
                    pe.wait_ge(S["z_done"], at(j * 12 + 2 * (k - 1) + c + 1))
                    pe.nop(nofuse=True)
                for a in (2 * c, 2 * c + 1):
                    ins = nc.tensor.transpose(psX[c][0:64, a % 2], Z[:, a, :], ident)
                ins.then_inc(S["t_mm"], 1)

            def p_level(j, k, c):
                pe.wait_ge(S["w_done_v"], at(j * 12 + 2 * k + c + 1))
                pe.wait_ge(S["x_bd"], at(j * 24 + 4 * (k - 1) + 2 * c + 2))
                for a in (2 * c, 2 * c + 1):
                    ins = mm(psP[c][:, a % 2], X[:, a, :], W[:, a, :], start=True, stop=True)
                ins.then_inc(S["p_mm"], 1)

            def m_level(j, par):
                pe.wait_ge(S["x_bd"], at(j * 24 + 24))
                pe.wait_ge(S["gq_done"], at(j + 1))
                for p in range(NP):
                    ins = mm(psM[:, p], X[:, p, :], GQ2[:, par, p, :], start=True, stop=True)
                ins.then_inc(S["m_mm"], 1)

            def outputs(j, last):
                pe.wait_ge(S["m_done"], at(j * 4 + 4))
                pe.wait_ge(S["gq_done"], at(j + 1 if last else j + 2))
                pe.wait_ge(S["t1_done"], at(j + 1 if last else j + 2))
                for n, dst in enumerate(PJ):
                    for p in range(NP):
                        ins = mm(dst[:, P * p:P * p + P], V[:, p, P * n:P * n + P], M[:, p, :], start=True, stop=True)
                    ins.then_inc(S["o_mm"], 1)

            def v_transposes(i, n):
                for dst in ((BA, BB)[n],):
                    pe.wait_ge(S["conv"], at(i * 12 + 9 + 3 * n))
                    if n == 1:
                        pe.wait_ge(S["m_done"], at(i * 4))
                    for p in range(NP):
                        ins = nc.tensor.transpose(dst[:, P * p:P * p + P], Y[:, 2 + n, P * p:P * p + P], ident)
                    ins.then_inc(S["vt_mm"], 1)

            def project_out(j, h, p, last):
                if p == 0:
                    pe.wait_ge(S["ot_done"], at(j * 2 + 2))
                for n in range(2):
                    ins = mm(AC[p // 2][:, E * (p % 2):E * (p % 2) + E], OT[:, n, P * p:P * p + P],
                             WO[:, ds(h * 2 + n, 1), :].rearrange("p o e -> p (o e)"), start=False, stop=(last and n == 1), skip_group_check=True)
                if p == NP - 1:
                    ins.then_inc(S["op_mm"], 1)

            with pe.Fori(0, G) as g:
                transposes(g * 3)
                pe.wait_ge(S["xl_done"], at(g * 4 + 2))
                for p in range(NP):
                    for n in range(2):
                        k = 0
                        for c in range(2):
                            for xt, wt in ((XH, ABH), (XL, ABH), (XH, ABL)):
                                o = P * p + 1 - n
                                ins = mm(BB[:, 32 * p + 16 * n:32 * p + 16 * n + 16], xt[:, c, o:o + P], wt[:, c, 16 * n:16 * n + 16],
                                         start=(k == 0), stop=(k == 5))
                                k += 1
                ins.then_inc(S["gate_mm"], 1)
                for p in range(NP):
                    pe.wait_ge(S["rha_done"], at(g * NP + p + 1))
                    if p:
                        pe.wait_ge(S["dec_exp"], at(g * 16 + 4 * p - 2))
                    for n, dst in enumerate((CA, CB)):
                        mm(dst[:, :], CST[:, C_UT:C_UT + 128], RHA[:, 8 * n:8 * n + 8, :].rearrange("p a t -> p (a t)"),
                           start=True, stop=True).then_inc(S["dec_mm"], 1)
                    pe.wait_ge(S["rhq_done"], at(g * NP + p + 1))
                    if p:
                        pe.wait_ge(S["dec_exp"], at(g * 16 + 4 * p))
                    for n, dst in enumerate((BA, BB)):
                        mm(dst[:, :], CST[:, C_LE:C_LE + 128], RHQ[:, 8 * n:8 * n + 8, :].rearrange("p a t -> p (a t)"),
                           start=True, stop=True).then_inc(S["dec_mm"], 1)
                for n in range(2):
                    mm(AC[n][:, :], ZW[:, :], XH[:, 0, 0:GT], start=True, stop=False, skip_group_check=True)
                it0 = g * NH
                pe.wait_ge(S["dec_exp"], at(g * 16 + 16))
                for b in range(4):
                    project(it0, 0, b, it0 * 2)
                v_transposes(it0, 0)
                v_transposes(it0, 1)
                grams(it0)
                norms(it0)
                spread_q(it0)

                def head(j, hj, par, i, hi, first=False):
                    def earlier(p):
                        if not first:
                            project_out(j - 1, hj - 1, p, False)

                    drained = j * 2 if first else j * 2 - 1
                    if i is not None:
                        project(i, hi, 0, drained, not first)
                    for k in range(1, LV):
                        for c in range(2):
                            w_level(j, k, c)
                            t_level(j, k, c)
                        if k == 5:
                            earlier(0)
                        elif i is not None:
                            if k <= 3:
                                project(i, hi, k, drained, not first)
                            else:
                                grams(i)
                        for c in range(2):
                            p_level(j, k, c)
                        if k == 4 and i is not None:
                            norms(i)
                        if k == 5:
                            earlier(1)
                    for c in range(2):
                        t_level(j, LV, c)
                    earlier(2)
                    if i is not None:
                        spread_q(i)
                    m_level(j, par)
                    earlier(3)
                    if i is not None:
                        for c in range(2):
                            w_level(i, 0, c)
                        v_transposes(i, 0)
                    outputs(j, i is None)
                    if i is not None:
                        v_transposes(i, 1)

                for c in range(2):
                    w_level(it0, 0, c)
                head(it0, 0, 0, it0 + 1, 1, first=True)
                with pe.Fori(0, NH // 2 - 1) as h2:
                    for odd in range(2):
                        h = h2 * 2 + 1 + odd
                        head(g * NH + h, h, 1 - odd, g * NH + h + 1, h + 1)
                head(g * NH + NH - 1, NH - 1, 1, None, None)
                for p in range(NP):
                    project_out(g * NH + NH - 1, NH - 1, p, True)

                pe.wait_ge(S["ld_ctx"], at(g * 48 + 48))
                for c, dst in enumerate((CA, CB)):
                    mm(dst[:, :], CST[0:64, C_REP + 128 * c:C_REP + 128 * c + 128], CT[:, :], start=True, stop=True).then_inc(S["rep_mm"], 1)
                transposes(g * 3 + 1)
                pe.wait_ge(S["xh_done"], at(g * 6 + 4))
                pe.wait_ge(S["kg_done"], at(g * 2 + 2))
                pe.wait_ge(S["vb_done"], at(g * 2 + 2))

                def scores(p):
                    pid = g * NP + p
                    for r, dst in enumerate((CA, CB, BA, BB)):
                        if p:
                            pe.wait_ge(S["sub_done"], at(pid * 4 + r - 3))
                        for c in range(2):
                            for n in range(2):
                                b = 2 * p + n
                                ins = mm(dst[64 * n:64 * n + 64, 256 * c:256 * c + 256], QT[32 * r:32 * r + 32, c, T * b:T * b + T],
                                         KG[32 * r:32 * r + 32, c, b].rearrange("p g t -> p (g t)"), start=True, stop=True, tile_position=(32 * r, 64 * n))
                        ins.then_inc(S["sc_mm"], 1)

                scores(0)
                for p in range(NP):
                    pid = g * NP + p
                    for r in range(4):
                        pe.wait_ge(S["exp_done"], at(pid * 4 + r + 1))
                        if r >= 2:
                            pe.wait_ge(S["pt_done"], at(pid * 4 + r - 1))
                        else:
                            pe.wait_ge(S["pt_done"], at(pid * 4))
                        for q in range(4):
                            ins = nc.tensor.transpose(PJ[r % 2][:, P * q:P * q + P], ES[:, q // 2, r, 2 * (q % 2):2 * (q % 2) + 2, :], ident)
                        ins.then_inc(S["pt_mm"], 1)
                    if p + 1 < NP:
                        scores(p + 1)
                    pe.wait_ge(S["pt_done"], at(pid * 4 + 4))
                    if p >= 2:
                        pe.wait_ge(S["nrm_done"], at(pid - 1))
                    for r in range(4):
                        for q in range(4):
                            kv = 4 * (q // 2) + r
                            for n in range(2):
                                b = 2 * p + n
                                col = (2 * kv + q % 2) * 18
                                ins = mm(AC[p % 2][64 * n:64 * n + 64, col:col + 18], PT[:, r, q, 64 * n:64 * n + 64],
                                         VB[:, 8 * b + kv].rearrange("p g d -> p (g d)"), start=True, stop=True)
                    ins.then_inc(S["pv_mm"], 1)

                transposes(g * 3 + 2)
                pe.wait_ge(S["xl_done"], at(g * 4 + 4))
                for f in range(FB):
                    if f >= 4:
                        pe.wait_ge(S["gelu_done"], at(g * FB + f - 3))
                    k = 0
                    for c in range(2):
                        for xt in (XH, XL):
                            ins = mm((CA, CB, BA, BB)[f % 4][:, :], W1[:, c, P * f:P * f + P], xt[:, c, 0:GT], start=(k == 0), stop=(k == 3))
                            k += 1
                    ins.then_inc(S["f1_mm"], 1)
                for f in range(FB):
                    pe.wait_ge(S["hl_done"], at(g * FB + f + 1))
                    for p in range(NP):
                        for k, ht in enumerate((HH, HL)):
                            ins = mm(AC[p // 2][:, E * (p % 2):E * (p % 2) + E], ht[:, f, P * p:P * p + P], W2[:, f, :],
                                     start=(f == 0 and k == 0 and p % 2 == 0), stop=(f == FB - 1 and k == 1), skip_group_check=True)
                ins.then_inc(S["f2_mm"], 1)


_NAMES = ["x", "ctxT", "ctxR", "wall", "wo", "wab", "cw", "w1", "b1", "w2", "b2", "cst"]


def kernel(**inp):
    import numpy as _np
    import concourse.bacc as _bacc
    from concourse import mybir as _mybir
    from concourse.bass_utils import run_bass_kernel_spmd as _run

    a = {k: _np.asarray(v) for k, v in inp.items()}
    x = a["x"].reshape(G, NP, P, E).transpose(0, 2, 1, 3)
    c = a["ctx_512"]
    ctxT = c.reshape(G, 8 * T, CD).transpose(0, 2, 1)
    ctxR = c.reshape(G, 8, T, CD).transpose(0, 2, 1, 3)
    wq = a["L0_attn_Wq"].reshape(E, NH, DK)
    wk = a["L0_attn_Wk"].reshape(E, NH, DK)
    wv = a["L0_attn_Wv"].reshape(E, NH, 2 * DK)
    wall = _np.concatenate([wq, wk, wv], axis=2).reshape(2, P, NH * 512)
    wo = a["L0_attn_Wo"].reshape(2 * NH, P, E).transpose(1, 0, 2)
    wab = _np.concatenate([a["L0_attn_Wa"], a["L0_attn_Wb"]], axis=1).reshape(2, P, 32).transpose(1, 0, 2)

    def taps(w, b, n):
        return _np.concatenate([w, b[:, None]], axis=1).reshape(NH, n, P, 5)

    cw = _np.concatenate([taps(a["L0_attn_qcw"], a["L0_attn_qcb"], 1), taps(a["L0_attn_kcw"], a["L0_attn_kcb"], 1),
                          taps(a["L0_attn_vcw"], a["L0_attn_vcb"], 2)], axis=1).transpose(2, 0, 1, 3).reshape(P, NH, 20)
    w1 = a["L0_ffn_w1"].T.reshape(2, P, F).transpose(1, 0, 2).reshape(P, 2 * F)
    w2 = a["L0_ffn_w2"].T.reshape(FB, P, E).transpose(1, 0, 2).reshape(P, FB * E)
    b1 = a["L0_ffn_b1"].reshape(FB, P).T
    b2 = _np.broadcast_to(a["L0_ffn_b2"][None, :], (P, E))
    vals = dict(x=x, ctxT=ctxT, ctxR=ctxR, wall=wall, wo=wo, wab=wab, cw=cw, w1=w1, b1=b1, w2=w2, b2=b2, cst=constants())

    nc = _bacc.Bacc("TRN2", target_bir_lowering=False, num_devices=1)
    arrays, args = {}, []
    for name in _NAMES:
        v = _np.ascontiguousarray(vals[name])
        arrays[f"in_{name}"] = v
        args.append(nc.dram_tensor(f"in_{name}", v.shape, _mybir.dt.from_np(v.dtype), kind="ExternalInput").ap())
    out = nc.dram_tensor("out", (G, P, NP, E), _mybir.dt.float32, kind="ExternalOutput").ap()
    build(nc, *args, out)
    r = _run(nc, [arrays], core_ids=[0])
    y = r.results[0]["out"]
    return y.transpose(0, 2, 1, 3).reshape(NB, T, E)
```

```python
from contextlib import ExitStack

import numpy as np
import concourse.bass as bass
from concourse import mybir

ALU = mybir.AluOpType
ACT = mybir.ActivationFunctionType
F32 = mybir.dt.float32
F16 = mybir.dt.float16
AX_X = mybir.AxisListType.X
ds = bass.ds

P = 128
T = 64
E = 256
NB = 64
GT = 512
G = NB * T // GT
NP = GT // P
NH = 16
DK = 128
LV = 6
CD = 64
F = 1024
FB = F // P
WS = 64.0
D8 = 8

C_ID, C_IC, C_MT = 0, 128, 192
C_UT, C_LE, C_ON = C_MT + 64 * LV, C_MT + 64 * LV + 128, C_MT + 64 * LV + 256
C_UTC = C_ON + 128
C_LEC, C_MA, C_MQ = C_UTC + 64, C_UTC + 128, C_UTC + 192
C_REP = C_MQ + 64
C_GM = C_REP + 256
C_ML = C_GM + 4
C_HI, C_LO = C_ML + 64, C_ML + 65
NCST = C_ML + 66


def constants():
    c = np.zeros((P, NCST), np.float32)
    p = np.arange(P)[:, None]
    q = np.arange(P)[None, :]
    s, j = p % T, np.arange(T)[None, :]
    same = (p // T) == (q // T)
    c[:, C_ID:C_ID + 128] = p == q
    c[:, C_IC:C_IC + 64] = s == j
    for k in range(LV):
        c[:, C_MT + 64 * k:C_MT + 64 * k + 64] = ((s >> (k + 1)) == (j >> (k + 1))) & ((s >> k) % 2 == 0) & ((j >> k) % 2 == 1)
    c[:, C_UT:C_UT + 128] = same & (p < q)
    c[:, C_LE:C_LE + 128] = same & (p >= q)
    c[:, C_ON:C_ON + 128] = same
    c[:, C_UTC:C_UTC + 64] = s < j
    c[:, C_LEC:C_LEC + 64] = s >= j
    c[:, C_MA:C_MA + 64] = s > j
    c[:, C_MQ:C_MQ + 64] = s <= j
    for half in range(2):
        for m in range(P):
            c[(half * 4 + m // 32) * D8 + m % D8, C_REP + 128 * half + m] = 1.0
    c[:, C_GM:C_GM + 4] = (p // D8) % 4 == np.arange(4)[None, :]
    c[:, C_ML:C_ML + 64] = (s % 2 == 1) & (j == s - 1)
    c[:, C_HI] = s[:, 0] >= T // 2
    c[:, C_LO] = s[:, 0] < T // 2
    return c


def build(nc, x, ctxT, ctxR, wall, wo, wab, cw, w1, b1, w2, b2, cst, out):
    ctx = ExitStack()
    with ctx:
        def sb(name, shape, dt=F32):
            return ctx.enter_context(nc.sbuf_tensor(name, shape, dt))

        def sem(name):
            return ctx.enter_context(nc.semaphore(name))

        WH = sb("WH", [P, 2, NH * 512], F16)
        WL = sb("WL", [P, 2, NH * 512], F16)
        WO = sb("WO", [P, 2 * NH, E])
        SCR = sb("SCR", [P, 8192])
        CST = sb("CST", [P, NCST])
        CW = sb("CW", [P, NH, 20])
        CWC = sb("CWC", [P, 20])
        AB32 = sb("AB32", [P, 2, 32])
        ABH = sb("ABH", [P, 2, 32], F16)
        ABL = sb("ABL", [P, 2, 32], F16)
        W1 = sb("W1", [P, 2, F], F16)
        W2 = sb("W2", [P, FB, E], F16)
        B1 = sb("B1", [P, FB])
        B2 = sb("B2", [P, E])
        XP = sb("XP", [P, NP, E])
        XC = sb("XC", [P, NP, E])
        XH = sb("XH", [P, 2, GT + 1], F16)
        XL = sb("XL", [P, 2, GT + 1], F16)
        STT6 = sb("STT6", [P, NP, 6])
        MV = sb("MV", [P, NP, 2])
        RSTD = sb("RSTD", [P, NP])
        VE = sb("VE", [P, NP])
        SSM = sb("SSM", [P, 2 * NP])
        MHALF = sb("MHALF", [P, 2 * NP])
        LA = sb("LA", [P, NP, NH])
        LT = sb("LT", [P, 4, NP, NH])
        BE = sb("BE", [P, NH, NP])
        KQ = sb("KQ", [P, 2, GT])
        Y = sb("Y", [P, 4, GT])
        V = sb("V", [P, NP, 256])
        SQ = sb("SQ", [P, 2, GT])
        XN = SQ[:, :, :].rearrange("p a (b e) -> p (a b) e", e=E)
        NQ = sb("NQ", [P, 2, NP])
        NBT = sb("NBT", [P, NP])
        RA = sb("RA", [P, NP])
        EAM = sb("EAM", [P, NP, T])
        EQM = sb("EQM", [P, NP, T])
        EAR = sb("EAR", [P, NP, T])
        A = sb("A", [P, NP, T])
        X = sb("X", [P, NP, T])
        X1L = sb("X1L", [P, NP, T])
        FK = sb("FK", [P, NP, T])
        M = sb("M", [P, NP, P])
        GQ2 = sb("GQ", [P, 2, NP, T])
        W = sb("W", [P, NP, T])
        Z = sb("Z", [P, NP, T])
        ZS = Z[:, 0:2, :].rearrange("p a (b n) -> p (a b) n", n=32)
        T12 = sb("T1", [P, 2, NP, T])
        DQ = sb("DQ", [P, NP, T])
        OT = sb("OT", [P, 2, GT])
        CT = sb("CT", [CD, GT])
        VT = sb("VT", [P, 8, CD])
        VB = sb("VB", [P, 64, 2, 9])
        MX = sb("MX", [P, 4, 8])
        RS = Z[:, 3, 0:32]
        OB = W[:, :, :].rearrange("p a t -> p (a t)").rearrange("p (n d) -> p n d", d=D8)
        SMALL = sb("SMALL", [P, 8])
        ONES = sb("ONES", [P, 1])
        ZW = sb("ZW", [P, P], F16)

        EA = SCR[:, 0:4096].rearrange("p (h a t) -> p h a t", h=NH, a=NP)
        EQ = SCR[:, 4096:8192].rearrange("p (h a t) -> p h a t", h=NH, a=NP)
        KG = SCR[:, 0:4096].rearrange("p (c b g t) -> p c b g t", c=2, b=8, g=4)
        ES = SCR[:, 4096:6144].rearrange("p (c r g t) -> p c r g t", c=2, r=4, g=4)
        PT = SCR[:, 6144:8192].rearrange("p (r q s) -> p r q s", r=4, q=4)
        H = SCR[:, 0:4096].rearrange("p (f t) -> p f t", f=FB)
        HH = SCR[:, 4096:6144].bitcast(F16).rearrange("p (f t) -> p f t", f=FB)
        HL = SCR[:, 6144:8192].bitcast(F16).rearrange("p (f t) -> p f t", f=FB)
        QT = KQ
        RHA = V[:, :, :].rearrange("p a (b t) -> p (a b) t", t=T)
        RHQ = OT[:, :, :].rearrange("p a (b t) -> p (a b) t", t=T)

        ident = CST[:, C_ID:C_ID + 128]
        identc = CST[:, C_IC:C_IC + 64]

        def mt(k):
            return CST[:, C_MT + 64 * k:C_MT + 64 * k + 64]

        def over_pairs(m, n=NP):
            return m[:, None, :].broadcast_to([P, n, T])

        PJ = [ctx.enter_context(nc.psum_tensor(f"PJ{i}", [P, GT], F32)) for i in range(2)]
        CA, CB, BA, BB = [ctx.enter_context(nc.psum_tensor(n, [P, GT], F32)) for n in ("CA", "CB", "BA", "BB")]
        AC = [ctx.enter_context(nc.psum_tensor(f"AC{i}", [P, GT], F32)) for i in range(2)]
        gram = PJ[0][:, :].rearrange("p (a k t) -> p a k t", a=NP, k=2)
        psR = PJ[1][:, 0:256].rearrange("p (a t) -> p a t", a=NP)
        psS = PJ[1][:, 256:256 + NP]
        psW = [b[:, 0:128].rearrange("p (a t) -> p a t", a=2) for b in (CA, CB)]
        psP = [b[:, 128:256].rearrange("p (a t) -> p a t", a=2) for b in (CA, CB)]
        psF = [b[:, 0:128].rearrange("p (a t) -> p a t", a=2) for b in (BA, BB)]
        psX = [b[:, 0:256].rearrange("p (a t) -> p a t", a=2) for b in (BA, BB)]

        def chain(c):
            return slice(2 * c, 2 * c + 2)

        names = """ld_const ld_wo ld_w0 ld_w1 ld_w2 ld_w3
            w_split w_hi tern_sum tern_all tern_done zeroed conv_scaled""".split()
        owned = {
            "sync": "ld_x ld_ctx st_out",
            "pool": "x1l_done x_first rhq_done masked rsq sq rstd vb_done",
            "act": "xh_done gate_s dec_exp tap kq x_copied f_done f_kept g_done ot_done v_done exp_done pt_done gelu_done",
            "dve": """ln_step xl_done gate_v rha_done cw_cur conv scale_done dq_done a_done gq_done t1_done w_done z_done o_sub m_done
                      x1_done kg_done mx_done sub_done rs_done ob_done nrm_done hh_done hl_done b2_done x3_done""",
            "pe": """tr_done gate_mm dec_mm proj gram_mm ss_mm r_mm w_mm t_mm p_mm f_mm g_mm m_mm o_mm vt_mm op_half op_mm
                     rep_mm sc_mm pt_mm pv_mm f1_mm f2_mm""",
        }
        names += " ".join(owned.values()).split()
        S = {n: sem(n) for n in names}
        LW = [S[f"ld_w{n}"] for n in range(4)]

        def start_counts(eng, who):
            for n in owned[who].split():
                eng.sem_inc(S[n], 1)

        def at(count):
            return count + 1

        block = ctx.enter_context(nc.Block())

        @block.sync
        def _(sp):
            start_counts(sp, "sync")
            sp.dma_start(CST[:, :], cst).then_inc(S["ld_const"], 16)
            sp.dma_start(CW[:, :, :], cw).then_inc(S["ld_const"], 16)
            sp.dma_start(AB32[:, :, :], wab).then_inc(S["ld_const"], 16)
            sp.dma_start(B1[:, :], b1).then_inc(S["ld_const"], 16)
            sp.dma_start(B2[:, :], b2).then_inc(S["ld_const"], 16)
            sp.dma_start(XP[:, :, :], x[0]).then_inc(S["ld_x"], 16)
            for n in range(8):
                if n >= 4:
                    sp.wait_ge(S["w_split"], n - 3)
                sp.dma_start(SCR[:, (n % 4) * 2048:(n % 4 + 1) * 2048],
                             wall[n // 4][:, (n % 4) * 2048:(n % 4 + 1) * 2048]).then_inc(LW[n % 4], 16)
            sp.wait_ge(S["w_split"], 6)
            sp.dma_start(SCR[:, 0:2048], w1).then_inc(LW[0], 16)
            sp.dma_start(SCR[:, 2048:4096], w2).then_inc(LW[1], 16)
            sp.dma_start(WO[:, :, :], wo).then_inc(S["ld_wo"], 16)

            def group(g, last):
                sp.wait_ge(S["kg_done"], at(g * 2))
                sp.wait_ge(S["vb_done"], at(g * 2))
                one = ds(g, 1)
                sp.dma_start(CT[:, :], ctxT[one].rearrange("a c t -> (a c) t")).then_inc(S["ld_ctx"], 16)
                sp.dma_start(VT[0:64, :, :], ctxR[one].rearrange("a t b c -> (a t) b c")).then_inc(S["ld_ctx"], 16)
                sp.dma_start(VT[64:128, :, :], ctxR[one].rearrange("a t b c -> (a t) b c")).then_inc(S["ld_ctx"], 16)
                sp.wait_ge(S["x1_done"], at(g * 2 + 2))
                sp.dma_start(XP[:, :, :], x[ds(G - 1 if last else g + 1, 1)].rearrange("a p n e -> (a p) n e")).then_inc(S["ld_x"], 16)
                sp.wait_ge(S["x3_done"], at(g * 2 + 2))
                sp.dma_start(out[one].rearrange("a p n e -> (a p) n e"), XC[:, :, :]).then_inc(S["st_out"], 16)

            with sp.Fori(0, G - 1) as g:
                group(g, False)
            group(G - 1, True)
            sp.wait_ge(S["st_out"], at(16 * G))

        @block.gpsimd
        def _(pool):
            start_counts(pool, "pool")
            pool.wait_ge(S["tern_sum"], 2)
            nc.gpsimd.partition_all_reduce(SMALL[:, 2:4], SMALL[:, 0:2], P, bass.bass_isa.ReduceOp.add).then_inc(S["tern_all"], 1)
            nc.gpsimd.memset(VB[:, :, :, :], 0.0).then_inc(S["zeroed"], 1)
            pool.wait_ge(S["zeroed"], 1)
            nc.gpsimd.memset(VB[:, :, :, 8:9], 0.0).then_inc(S["zeroed"], 1)
            pool.wait_ge(S["zeroed"], 2)
            nc.gpsimd.memset(VB[0:64, :, 0, 8:9], 1.0).then_inc(S["zeroed"], 1)
            pool.wait_ge(S["zeroed"], 3)
            nc.gpsimd.memset(VB[64:128, :, 1, 8:9], 1.0).then_inc(S["zeroed"], 1)
            pool.wait_ge(S["zeroed"], 4)
            nc.gpsimd.memset(MHALF[:, :], -0.5).then_inc(S["zeroed"], 1)
            pool.wait_ge(S["zeroed"], 5)
            pool.wait_ge(S["ld_const"], 80)

            def rstd(nid):
                pool.wait_ge(S["ln_step"], at(nid * 13 + 9))
                nc.gpsimd.tensor_tensor(RSTD[:, :], VE[:, :], MHALF[:, 0:NP], ALU.pow).then_inc(S["rstd"], 1)

            def inverse_norms(it):
                pool.wait_ge(S["scale_done"], at(it * 7 + 4))
                nc.gpsimd.tensor_tensor(NQ[:, :, :].rearrange("p k a -> p (k a)"), SSM[:, :], MHALF[:, :], ALU.pow).then_inc(S["rsq"], 1)

            def masked(it, h):
                pool.wait_ge(S["scale_done"], at(it * 7))
                nc.gpsimd.tensor_tensor(EAM[:, :, :], EA[:, ds(h, 1), :, :].rearrange("p o a t -> p (o a) t"),
                                        over_pairs(CST[:, C_MA:C_MA + 64]), ALU.mult).then_inc(S["masked"], 1)
                pool.wait_ge(S["gq_done"], at(it))
                nc.gpsimd.tensor_tensor(EQM[:, :, :], EQ[:, ds(h, 1), :, :].rearrange("p o a t -> p (o a) t"),
                                        over_pairs(CST[:, C_MQ:C_MQ + 64]), ALU.mult).then_inc(S["masked"], 1)

            def squares(it):
                pool.wait_ge(S["ss_mm"], at(it))
                pool.wait_ge(S["kq"], at(it * 2 + 1))
                nc.gpsimd.tensor_tensor(SQ[:, 0, :], KQ[:, 1, :], KQ[:, 1, :], ALU.mult).then_inc(S["sq"], 1)

            def x_first(it):
                pool.wait_ge(S["a_done"], at(it + 1))
                nc.gpsimd.tensor_tensor(X1L[:, :, :], A[:, :, :], over_pairs(CST[:, C_ML:C_ML + 64]), ALU.mult).then_inc(S["x1l_done"], 1)
                pool.wait_ge(S["x1l_done"], at(it + 1))
                pool.wait_ge(S["m_mm"], at(it * 2))
                nc.gpsimd.tensor_tensor(X[:, :, :], over_pairs(identc), X1L[:, :, :], ALU.subtract).then_inc(S["x_first"], 1)

            rstd(0)
            with pool.Fori(0, G) as g:
                pool.wait_ge(S["gate_v"], at(g * 6 + 6))
                for p in range(NP):
                    if p:
                        pool.wait_ge(S["dec_mm"], at(g * 16 + 4 * p))
                    nc.gpsimd.tensor_tensor(RHQ, CST[:, C_UTC:C_UTC + 64][:, None, :].broadcast_to([P, NH, T]),
                                            LA[:, p, :][:, :, None].broadcast_to([P, NH, T]), ALU.mult).then_inc(S["rhq_done"], 1)
                squares(g * NH)
                pool.wait_ge(S["dec_exp"], at(g * 16 + 16))
                masked(g * NH, 0)
                inverse_norms(g * NH)
                x_first(g * NH)
                with pool.Fori(1, NH) as h:
                    masked(g * NH + h, h)
                    squares(g * NH + h)
                    inverse_norms(g * NH + h)
                    x_first(g * NH + h)
                pool.wait_ge(S["ld_ctx"], at(g * 48 + 48))
                pool.wait_ge(S["pv_mm"], at(g * 4))
                pool.nop(nofuse=True)
                for n in range(2):
                    pool.wait_ge(S["vb_done"], at(g * 2 + n))
                    pool.nop(nofuse=True)
                    nc.gpsimd.tensor_copy(VB[64 * n:64 * n + 64, :, n, 0:8],
                                          VT[64 * n:64 * n + 64, :, :].rearrange("p b (k d) -> p (b k) d", d=D8)).then_inc(S["vb_done"], 1)
                pool.wait_ge(S["vb_done"], at(g * 2 + 2))
                rstd(g * 3 + 1)
                rstd(g * 3 + 2)
                rstd(g * 3 + 3)

        @block.scalar
        def _(act):
            start_counts(act, "act")
            for n in range(8):
                act.wait_ge(LW[n % 4], 16 * (n // 4 + 1))
                nc.scalar.activation(WH[:, n // 4, (n % 4) * 2048:(n % 4 + 1) * 2048], SCR[:, (n % 4) * 2048:(n % 4 + 1) * 2048],
                                     ACT.Copy, scale=WS).then_inc(S["w_hi"], 1)

            def transposed(nid, n):
                for c in range(2):
                    act.wait_ge(S["tr_done"], at(nid * 2 + c + 1))
                    if n == 1:
                        nc.scalar.activation(QT[:, c, :], PJ[c][:, :], ACT.Copy).then_inc(S["xh_done"], 1)
                    else:
                        nc.scalar.activation(XH[:, c, 0:GT], PJ[c][:, :], ACT.Copy).then_inc(S["xh_done"], 1)

            def tap(it, b):
                act.wait_ge(S["proj"], at(it * 4 + b + 1))
                act.wait_ge(S["cw_cur"], at(it + 1))
                act.wait_ge(S["vt_mm"], at(it * 2))
                act.wait_ge(S["kq"], at(it * 2))
                nc.scalar.activation(Y[:, b, :], PJ[b % 2][:, :], ACT.Identity, scale=CWC[:, 5 * b + 3:5 * b + 4],
                                     bias=CWC[:, 5 * b + 4:5 * b + 5]).then_inc(S["tap"], 1)

            def silu_kq(it, b):
                act.wait_ge(S["conv"], at(it * 12 + 3 * b + 3))
                act.wait_ge(S["gram_mm"], at(it))
                act.wait_ge(S["sq"], at(it))
                nc.scalar.activation(KQ[:, 1 - b, :], Y[:, b, :], ACT.Silu).then_inc(S["kq"], 1)

            def silu_v(it, b):
                act.wait_ge(S["vt_mm"], at(it * 2 + b - 1))
                act.wait_ge(S["o_mm"], at(it * 2))
                nc.scalar.activation(V[:, :, (b - 2) * P:(b - 1) * P], (BA, BB)[b - 2][:, :].rearrange("p (a n) -> p a n", a=NP),
                                     ACT.Silu).then_inc(S["v_done"], 1)

            def x_copy(it, k, c):
                act.wait_ge(S["t_mm"], at(it * 8 + 2 * (k - 2) + c + 1))
                act.wait_ge(S["p_mm"], at(it * 8 + 2 * (k - 2) + c + 1))
                for n in range(2):
                    lo = 64 * n
                    nc.scalar.activation(X[lo:lo + 64, chain(c), :], psX[c][0:64, :, lo:lo + 64], ACT.Copy).then_inc(S["x_copied"], 1)

            def f_lower(j, c):
                act.wait_ge(S["f_mm"], at(j * 2 + c + 1))
                act.wait_ge(S["t_mm"], at(j * 8 + 8))
                nc.scalar.activation(Z[:, chain(c), :], psF[c], ACT.Copy, scale=CST[:, C_HI:C_HI + 1]).then_inc(S["f_done"], 1)

            def f_keep(j, c):
                act.wait_ge(S["m_done"], at(j * 4))
                nc.scalar.activation(FK[:, chain(c), :], psF[c], ACT.Copy).then_inc(S["f_kept"], 1)

            def g_upper(j, c):
                act.wait_ge(S["g_mm"], at(j * 2 + c + 1))
                nc.scalar.activation(W[:, chain(c), :], psW[c], ACT.Copy, scale=CST[:, C_LO:C_LO + 1]).then_inc(S["g_done"], 1)

            def o_out(it):
                for n, src in enumerate(PJ):
                    act.wait_ge(S["o_mm"], at(it * 2 + n + 1))
                    act.wait_ge(S["op_mm"], at(it))
                    nc.scalar.activation(OT[:, n, :], src[:, :], ACT.Copy).then_inc(S["ot_done"], 1)

            act.wait_ge(S["ld_const"], 80)

            def gates(g):
                act.wait_ge(S["gate_v"], at(g * 6 + 3))
                nc.scalar.activation(LT[:, 2], LT[:, 0], ACT.Exp, scale=-1.0).then_inc(S["gate_s"], 1)
                nc.scalar.activation(LT[:, 3], ZS[:, :, 16:32], ACT.Exp, scale=-1.0).then_inc(S["gate_s"], 1)
                act.wait_ge(S["gate_v"], at(g * 6 + 4))
                act.wait_ge(S["gate_s"], at(g * 3 + 1))
                nc.scalar.activation(LT[:, 0], LT[:, 2], ACT.Ln).then_inc(S["gate_s"], 1)

            def decays(g, p):
                for n, src in enumerate((CA, CB, BA, BB)):
                    act.wait_ge(S["dec_mm"], at(g * 16 + 4 * p + n + 1))
                    act.wait_ge(S["f2_mm"], at(g))
                    dst = (EA if n < 2 else EQ)[:, (n % 2) * 8:(n % 2) * 8 + 8, p, :]
                    nc.scalar.activation(dst, src[:, :].rearrange("p (h t) -> p h t", h=8), ACT.Exp).then_inc(S["dec_exp"], 1)

            transposed(0, 0)
            gates(0)
            with act.Fori(0, G) as g:
                it0 = g * NH
                tap(it0, 0)
                tap(it0, 1)
                decays(g, 0)
                decays(g, 1)
                tap(it0, 2)
                decays(g, 2)
                tap(it0, 3)
                silu_kq(it0, 0)
                silu_kq(it0, 1)
                decays(g, 3)
                silu_v(it0, 2)
                silu_v(it0, 3)

                def head(j, i):
                    if i is not None:
                        tap(i, 0)
                    for k in range(1, LV):
                        if k > 1:
                            x_copy(j, k, 0)
                            x_copy(j, k, 1)
                        if i is not None:
                            if k <= 3:
                                tap(i, k)
                            if k <= 2:
                                silu_kq(i, k - 1)
                    for step in (f_lower, f_keep, g_upper):
                        for c in range(2):
                            step(j, c)
                    o_out(j)
                    if i is not None:
                        silu_v(i, 2)
                        silu_v(i, 3)

                head(it0, it0 + 1)
                with act.Fori(1, NH - 1) as h:
                    head(g * NH + h, g * NH + h + 1)
                head(g * NH + NH - 1, None)

                transposed(g * 3 + 1, 1)
                for p in range(NP):
                    pid = g * NP + p
                    for r in range(4):
                        act.wait_ge(S["sub_done"], at(pid * 4 + r + 1))
                        nc.scalar.activation(ES[:, :, r], ES[:, :, r], ACT.Exp, scale=float(D8) ** -0.5).then_inc(S["exp_done"], 1)
                    for r in range(4):
                        act.wait_ge(S["pt_mm"], at(pid * 4 + r + 1))
                        act.wait_ge(S["pv_mm"], at(pid))
                        nc.scalar.activation(PT[:, r], PJ[r % 2][:, :].rearrange("p (q s) -> p q s", q=4), ACT.Copy).then_inc(S["pt_done"], 1)
                transposed(g * 3 + 2, 2)
                for f in range(FB):
                    act.wait_ge(S["f1_mm"], at(g * FB + f + 1))
                    nc.scalar.activation(H[:, f, :], (CA, CB, BA, BB)[f % 4][:, :], ACT.Gelu, bias=B1[:, f:f + 1]).then_inc(S["gelu_done"], 1)
                transposed(g * 3 + 3, 0)
                gates(g + 1)

        @block.vector
        def _(dve):
            start_counts(dve, "dve")
            V_ = nc.vector
            for n in range(8):
                dve.wait_ge(S["w_hi"], n + 1)
                sl = slice((n % 4) * 2048, (n % 4 + 1) * 2048)
                V_.scalar_tensor_tensor(WL[:, n // 4, sl], SCR[:, sl], WS, WH[:, n // 4, sl], ALU.mult, ALU.subtract).then_inc(S["w_split"], 1)
            dve.wait_ge(S["ld_const"], 80)
            V_.tensor_copy(ABH[:, :, :], AB32[:, :, :]).then_inc(S["conv_scaled"], 1)
            cwv = CW[:, :, :].rearrange("p h (b n) -> p (h b) n", n=5)[:, :, 0:4]
            V_.tensor_scalar(cwv, cwv, 1.0 / WS, None, ALU.mult).then_inc(S["conv_scaled"], 1)
            dve.wait_ge(S["conv_scaled"], 2)
            V_.tensor_tensor(ABL[:, :, :], AB32[:, :, :], ABH[:, :, :], ALU.subtract).then_inc(S["conv_scaled"], 1)
            V_.memset(M[:, :, :], 0.0).then_inc(S["conv_scaled"], 1)
            V_.memset(ONES[:, :], 1.0).then_inc(S["conv_scaled"], 1)
            V_.memset(ZW[:, :], 0.0).then_inc(S["conv_scaled"], 1)
            V_.memset(XH[:, :, GT:GT + 1], 0.0).then_inc(S["conv_scaled"], 1)
            V_.memset(XL[:, :, GT:GT + 1], 0.0).then_inc(S["conv_scaled"], 1)
            dve.wait_ge(LW[0], 48)
            dve.wait_ge(LW[1], 48)
            for n in range(2):
                V_.tensor_reduce(SMALL[:, n:n + 1], SCR[:, 2048 * n:2048 * n + 2048], AX_X, ALU.add,
                                 apply_absolute_value=True).then_inc(S["tern_sum"], 1)
            dve.wait_ge(S["tern_all"], 1)
            V_.tensor_scalar(SMALL[:, 4:6], SMALL[:, 2:4], 1.0 / (E * F), 1e-8, ALU.mult, ALU.max).then_inc(S["tern_done"], 1)
            dve.wait_ge(S["tern_done"], 1)
            V_.tensor_scalar(SMALL[:, 6:8], SMALL[:, 4:6], -0.5, None, ALU.mult).then_inc(S["tern_done"], 1)
            V_.tensor_scalar(SMALL[:, 0:2], SMALL[:, 4:6], 0.5, None, ALU.mult).then_inc(S["tern_done"], 1)
            dve.wait_ge(S["tern_done"], 3)
            for n, dst in enumerate((W1[:, :, :].rearrange("p c f -> p (c f)"), W2[:, :, :].rearrange("p f e -> p (f e)"))):
                w = SCR[:, 2048 * n:2048 * n + 2048]
                V_.tensor_scalar(SCR[:, 4096 + 2048 * n:6144 + 2048 * n], w, SMALL[:, 6 + n:7 + n], None, ALU.is_lt).then_inc(S["tern_done"], 1)
                dve.wait_ge(S["tern_done"], 4 + 2 * n)
                V_.scalar_tensor_tensor(dst, w, SMALL[:, n:n + 1], SCR[:, 4096 + 2048 * n:6144 + 2048 * n], ALU.is_gt, ALU.subtract).then_inc(S["tern_done"], 1)

            def pair_stats(nid, src, pairs):
                dve.wait_ge(S["ln_step"], at(nid * 13))
                for p in pairs:
                    V_.bn_stats(STT6[:, p, :], src[:, p, :]).then_inc(S["ln_step"], 1)

            def norm_stats(nid):
                dve.wait_ge(S["ln_step"], at(nid * 13 + 4))
                dve.nop(nofuse=True)
                for p in range(NP):
                    V_.bn_aggr(MV[:, p, :], STT6[:, p, :]).then_inc(S["ln_step"], 1)
                dve.wait_ge(S["ln_step"], at(nid * 13 + 8))
                V_.tensor_scalar(VE[:, :], MV[:, :, 1], 1e-5, None, ALU.add).then_inc(S["ln_step"], 1)

            def norm_apply(nid, src):
                dve.wait_ge(S["rstd"], at(nid + 1))
                dve.wait_ge(S["tr_done"], at(nid * 2))
                for p in range(NP):
                    V_.tensor_scalar(XN[:, p, :], src[:, p, :], MV[:, p, 0:1], RSTD[:, p:p + 1], ALU.subtract, ALU.mult).then_inc(S["ln_step"], 1)

            def norm(nid, src):
                pair_stats(nid, src, range(NP))
                norm_stats(nid)
                norm_apply(nid, src)

            def low_parts(nid):
                for c in range(2):
                    dve.wait_ge(S["xh_done"], at(nid * 2 + c + 1))
                    V_.tensor_tensor(XL[:, c, 0:GT], PJ[c][:, :], XH[:, c, 0:GT], ALU.subtract).then_inc(S["xl_done"], 1)

            def cw_cur(it, h):
                dve.wait_ge(S["tap"], at(it * 4))
                dve.wait_ge(S["conv"], at(it * 12))
                V_.tensor_copy(CWC[:, :], CW[:, ds(h, 1), :].rearrange("p o n -> p (o n)")).then_inc(S["cw_cur"], 1)
                dve.wait_ge(S["cw_cur"], at(it + 1))

            def conv(it, b, m):
                if m == 1:
                    dve.wait_ge(S["tap"], at(it * 4 + b + 1))
                else:
                    dve.wait_ge(S["conv"], at(it * 12 + 3 * b + m - 1))
                yv = Y[:, b, :].rearrange("p (n t) -> p n t", t=T)
                pv = PJ[b % 2][:, :].rearrange("p (n t) -> p n t", t=T)
                V_.scalar_tensor_tensor(yv[:, :, m:T], pv[:, :, 0:T - m], CWC[:, 5 * b + 3 - m:5 * b + 4 - m], yv[:, :, m:T],
                                        ALU.mult, ALU.add).then_inc(S["conv"], 1)

            def squared_norms(j):
                dve.wait_ge(S["gram_mm"], at(j + 1))
                dve.wait_ge(S["r_mm"], at(j))
                V_.tensor_tensor(DQ[:, :, :], gram[:, :, 0, :], over_pairs(identc), ALU.mult).then_inc(S["scale_done"], 1)
                dve.wait_ge(S["scale_done"], at(j * 7 + 1))
                V_.tensor_reduce(SSM[:, 0:NP], DQ[:, :, :], AX_X, ALU.add).then_inc(S["scale_done"], 1)
                dve.wait_ge(S["scale_done"], at(j * 7 + 2))
                V_.tensor_scalar(SSM[:, 0:NP], SSM[:, 0:NP], 1e-24, None, ALU.max).then_inc(S["scale_done"], 1)
                dve.wait_ge(S["ss_mm"], at(j + 1))
                V_.tensor_scalar(SSM[:, NP:2 * NP], psS, 1e-24, None, ALU.max).then_inc(S["scale_done"], 1)

            def decayed(j, par):
                dve.wait_ge(S["masked"], at(j * 2 + 2))
                dve.wait_ge(S["a_done"], at(j))
                V_.tensor_tensor(EAR[:, :, :], gram[:, :, 0, :], EAM[:, :, :], ALU.mult).then_inc(S["scale_done"], 1)
                V_.tensor_tensor(GQ2[:, par], gram[:, :, 1, :], EQM[:, :, :], ALU.mult).then_inc(S["gq_done"], 1)

            def scales(j, h):
                dve.wait_ge(S["rsq"], at(j + 1))
                dve.wait_ge(S["t1_done"], at(j))
                V_.tensor_tensor(NBT[:, :], NQ[:, 0, :], BE[:, ds(h, 1), :].rearrange("p o a -> p (o a)"), ALU.mult).then_inc(S["scale_done"], 1)
                V_.tensor_tensor(DQ[:, :, :], over_pairs(identc), NQ[:, 1, :][:, :, None].broadcast_to([P, NP, T]), ALU.mult).then_inc(S["dq_done"], 1)
                dve.wait_ge(S["scale_done"], at(j * 7 + 6))
                V_.tensor_tensor(RA[:, :], NBT[:, :], NQ[:, 0, :], ALU.mult).then_inc(S["scale_done"], 1)

            def a_matrix(j):
                dve.wait_ge(S["scale_done"], at(j * 7 + 7))
                dve.wait_ge(S["g_mm"], at(j * 2))
                V_.tensor_tensor(A[:, :, :], EAR[:, :, :], RA[:, :][:, :, None].broadcast_to([P, NP, T]), ALU.mult).then_inc(S["a_done"], 1)

            def query_scales(j, par):
                dve.wait_ge(S["r_mm"], at(j + 1))
                V_.tensor_tensor(T12[:, par], psR, NBT[:, :][:, :, None].broadcast_to([P, NP, T]), ALU.mult).then_inc(S["t1_done"], 1)

            def w_masked(j, k, c):
                dve.wait_ge(S["w_mm"], at(j * 10 + 2 * k + c + 1))
                if k == 0:
                    dve.wait_ge(S["m_mm"], at(j * 2))
                V_.tensor_tensor(W[:, chain(c), :], psW[c], over_pairs(mt(k), 2), ALU.mult).then_inc(S["w_done"], 1)

            def z_next(j, k, c):
                zc = Z[:, chain(c), :]
                if k == 0:
                    dve.wait_ge(S["w_done"], at(j * 10 + c + 1))
                    dve.wait_ge(S["g_mm"], at(j * 2))
                    V_.tensor_tensor(zc, over_pairs(identc, 2), W[:, chain(c), :], ALU.subtract).then_inc(S["z_done"], 1)
                else:
                    dve.wait_ge(S["z_done"], at(j * 10 + 2 * (k - 1) + c + 1))
                    dve.wait_ge(S["p_mm"], at(j * 8 + 2 * (k - 1) + c + 1))
                    V_.tensor_tensor(zc, zc, psP[c], ALU.subtract).then_inc(S["z_done"], 1)

            def m_product(j):
                for c in range(2):
                    dve.wait_ge(S["m_mm"], at(j * 2 + c + 1))
                    dve.wait_ge(S["f_kept"], at(j * 2 + c + 1))
                    V_.tensor_tensor(FK[:, chain(c), :], FK[:, chain(c), :], psP[c], ALU.subtract).then_inc(S["o_sub"], 1)

            def m_scaled(j, par):
                dve.wait_ge(S["t1_done"], at(j + 1))
                dve.wait_ge(S["o_mm"], at(j * 2))
                for c in range(2):
                    dve.wait_ge(S["o_sub"], at(j * 2 + c + 1))
                    for n in range(2):
                        lo = 64 * n
                        V_.tensor_tensor(M[lo:lo + 64, chain(c), lo:lo + 64], FK[lo:lo + 64, chain(c), :], T12[lo:lo + 64, par, chain(c), :],
                                         ALU.mult).then_inc(S["m_done"], 1)

            def gates_in(g):
                dve.wait_ge(S["gate_mm"], at(g + 1))
                V_.tensor_copy(ZS[:, :, :], BB[:, 0:128].rearrange("p (a n) -> p a n", a=NP)).then_inc(S["gate_v"], 1)
                dve.wait_ge(S["gate_v"], at(g * 6 + 1))
                V_.scalar_tensor_tensor(LT[:, 0], ZS[:, :, 0:16], -1.0, ZS[:, :, 0:16], ALU.mult, ALU.max).then_inc(S["gate_v"], 1)
                V_.tensor_scalar(LT[:, 1], ZS[:, :, 0:16], 0.0, None, ALU.min).then_inc(S["gate_v"], 1)

            def gates_out(g):
                dve.wait_ge(S["gate_s"], at(g * 3 + 2))
                V_.tensor_scalar(LT[:, 2:4], LT[:, 2:4], 1.0, None, ALU.add).then_inc(S["gate_v"], 1)
                dve.wait_ge(S["gate_v"], at(g * 6 + 4))
                V_.reciprocal(BE[:, :, :].rearrange("p h a -> p a h"), LT[:, 3]).then_inc(S["gate_v"], 1)
                dve.wait_ge(S["gate_s"], at(g * 3 + 3))
                V_.tensor_tensor(LA[:, :, :], LT[:, 1], LT[:, 0], ALU.subtract).then_inc(S["gate_v"], 1)
                dve.wait_ge(S["gate_v"], at(g * 6 + 6))

            def decay_rows(g, p):
                if p:
                    dve.wait_ge(S["dec_mm"], at(g * 16 + 4 * p - 2))
                V_.tensor_tensor(RHA, CST[:, C_LEC:C_LEC + 64][:, None, :].broadcast_to([P, NH, T]),
                                 LA[:, p, :][:, :, None].broadcast_to([P, NH, T]), ALU.mult).then_inc(S["rha_done"], 1)

            dve.wait_ge(S["ld_x"], at(16))
            norm(0, XP)
            low_parts(0)
            gates_in(0)
            gates_out(0)
            with dve.Fori(0, G) as g:
                it0 = g * NH
                cw_cur(it0, 0)
                for b in range(4):
                    decay_rows(g, b)
                    for m in (1, 2, 3):
                        conv(it0, b, m)

                squared_norms(it0)
                decayed(it0, 0)
                scales(it0, 0)
                a_matrix(it0)
                query_scales(it0, 0)

                after_w = [[], [(0, 1), (0, 2)], [(1, 2), (1, 3)], [(2, 2), (2, 3)], [(3, 2), (3, 3)], []]
                after_z = [[], [(0, 3), (1, 1)], [(2, 1)], [(3, 1)], [], []]

                def head(j, par, i, hi):
                    if i is not None:
                        cw_cur(i, hi)
                    for k in range(LV - 1):
                        for c in range(2):
                            w_masked(j, k, c)
                        if i is not None:
                            for b, m in after_w[k]:
                                conv(i, b, m)
                        for c in range(2):
                            z_next(j, k, c)
                        if i is not None:
                            for b, m in after_z[k]:
                                conv(i, b, m)
                    if i is not None:
                        squared_norms(i)
                        decayed(i, 1 - par)
                    if i is not None:
                        scales(i, hi)
                        a_matrix(i)
                    m_product(j)
                    if i is not None:
                        query_scales(i, 1 - par)
                    m_scaled(j, par)

                head(it0, 0, it0 + 1, 1)
                with dve.Fori(0, NH // 2 - 1) as h2:
                    for odd in range(2):
                        h = h2 * 2 + 1 + odd
                        head(g * NH + h, 1 - odd, g * NH + h + 1, h + 1)
                head(g * NH + NH - 1, 1, None, None)

                for c, src in enumerate((CA, CB)):
                    dve.wait_ge(S["rep_mm"], at(g * 2 + c + 1))
                    for b in range(8):
                        ins = V_.tensor_tensor(KG[:, c, b], src[:, T * b:T * b + T][:, None, :].broadcast_to([P, 4, T]),
                                               CST[:, C_GM:C_GM + 4][:, :, None].broadcast_to([P, 4, T]), ALU.mult)
                    ins.then_inc(S["kg_done"], 1)

                dve.wait_ge(S["st_out"], at(g * 16))
                for n in range(2):
                    if n == 0:
                        dve.wait_ge(S["op_half"], at(g + 1))
                    else:
                        dve.wait_ge(S["op_mm"], at(g * NH + NH))
                    xv, xo = (b[:, 2 * n:2 * n + 2, :].rearrange("p a e -> p (a e)") for b in (XC, XP))
                    V_.tensor_tensor(xv, AC[n][:, :], xo, ALU.add).then_inc(S["x1_done"], 1)
                    dve.wait_ge(S["x1_done"], at(g * 2 + n + 1))
                    pair_stats(g * 3 + 1, XC, (2 * n, 2 * n + 1))
                norm_stats(g * 3 + 1)
                norm_apply(g * 3 + 1, XC)

                def softmax_in(p):
                    pid = g * NP + p
                    for r, src in enumerate((CA, CB, BA, BB)):
                        sv = src[:, :].rearrange("p (c g t) -> p c g t", c=2, g=4)
                        dve.wait_ge(S["sc_mm"], at(pid + 1))
                        dve.wait_ge(S["sub_done"], at(pid * 4 + r))
                        V_.tensor_reduce(MX[:, r, :], src[:, :].rearrange("p (n t) -> p n t", t=T), AX_X, ALU.max).then_inc(S["mx_done"], 1)
                        dve.wait_ge(S["mx_done"], at(pid * 4 + r + 1))
                        if r == 0:
                            dve.wait_ge(S["pt_mm"], at(pid * 4))
                        V_.tensor_tensor(ES[:, :, r], sv, MX[:, r, :].rearrange("p (c g) -> p c g", c=2)[:, :, :, None].broadcast_to([P, 2, 4, T]),
                                         ALU.subtract).then_inc(S["sub_done"], 1)

                def softmax_out(p):
                    pid = g * NP + p
                    pv = AC[p % 2][:, 0:288].rearrange("p (n d) -> p n d", d=9)
                    dve.wait_ge(S["pv_mm"], at(pid + 1))
                    dve.wait_ge(S["ob_done"], at(pid))
                    V_.reciprocal(RS[:, :], pv[:, :, 8]).then_inc(S["rs_done"], 1)
                    dve.wait_ge(S["rs_done"], at(pid + 1))
                    dve.wait_ge(S["nrm_done"], at(pid))
                    V_.tensor_tensor(OB[:, :, :], pv[:, :, 0:8], RS[:, :][:, :, None].broadcast_to([P, 32, D8]), ALU.mult).then_inc(S["ob_done"], 1)
                    dve.wait_ge(S["ob_done"], at(pid + 1))
                    V_.tensor_tensor(XC[:, p, :], XC[:, p, :], OB[:, :, :].rearrange("p n d -> p (n d)"), ALU.add).then_inc(S["nrm_done"], 1)

                for p in range(NP):
                    softmax_in(p)
                    if p:
                        softmax_out(p - 1)
                softmax_out(NP - 1)
                dve.wait_ge(S["nrm_done"], at(g * NP + NP))
                norm(g * 3 + 2, XC)
                low_parts(g * 3 + 2)
                dve.wait_ge(S["ld_x"], at(g * 16 + 32))
                pair_stats(g * 3 + 3, XP, range(NP))
                norm_stats(g * 3 + 3)
                for f in range(FB):
                    if f == 3:
                        norm_apply(g * 3 + 3, XP)
                    if f == 7:
                        low_parts(g * 3 + 3)
                    dve.wait_ge(S["gelu_done"], at(g * FB + f + 1))
                    V_.tensor_copy(HH[:, f, :], H[:, f, :]).then_inc(S["hh_done"], 1)
                    dve.wait_ge(S["hh_done"], at(g * FB + f + 1))
                    V_.tensor_tensor(HL[:, f, :], H[:, f, :], HH[:, f, :], ALU.subtract).then_inc(S["hl_done"], 1)
                dve.wait_ge(S["ln_step"], at(g * 39 + 39))
                for n in range(2):
                    xv = XC[:, 2 * n:2 * n + 2, :]
                    V_.tensor_tensor(xv, xv, B2[:, :][:, None, :].broadcast_to([P, 2, E]), ALU.add).then_inc(S["b2_done"], 1)
                gates_in(g + 1)
                dve.wait_ge(S["f2_mm"], at(g + 1))
                for n in range(2):
                    xv = XC[:, 2 * n:2 * n + 2, :]
                    dve.wait_ge(S["b2_done"], at(g * 2 + n + 1))
                    V_.tensor_tensor(xv, AC[n][:, :].rearrange("p (a e) -> p a e", a=2), xv, ALU.add).then_inc(S["x3_done"], 1)
                gates_out(g + 1)

        @block.tensor
        def _(pe):
            start_counts(pe, "pe")
            mm = nc.tensor.matmul
            pe.wait_ge(S["ld_const"], 80)
            pe.wait_ge(S["conv_scaled"], 8)
            pe.wait_ge(S["tern_done"], 7)
            pe.wait_ge(S["zeroed"], 4)
            pe.wait_ge(S["w_hi"], 8)
            pe.wait_ge(S["ld_wo"], 16)

            def transposes(nid):
                pe.wait_ge(S["ln_step"], at(nid * 13 + 13))
                for c in range(2):
                    for p in range(NP):
                        ins = nc.tensor.transpose(PJ[c][:, P * p:P * p + P], XN[:, p, P * c:P * c + P], ident)
                    ins.then_inc(S["tr_done"], 1)

            def per_batch(dst, lhsT, rhs):
                for n in range(2):
                    b = slice(64 * n, 64 * n + 64)
                    ins = mm(dst[b], lhsT[b, :], rhs[b], start=True, stop=True, tile_position=(64 * n, 64 * n))
                return ins

            TERMS = [(WH, XH), (WH, XL), (WL, XH)]

            def project(it, h, b, drained=None, inner=False):
                if b >= 2:
                    pe.wait_ge(S["conv"], at(it * 12 + 3 * b - 3))
                else:
                    pe.wait_ge(S["ot_done"], at(drained + b if inner else drained))
                    pe.wait_ge(S["gq_done"], at(it))
                    pe.wait_ge(S["t1_done"], at(it))
                n = 0
                for c in range(2):
                    for wt, xt in TERMS:
                        ins = mm(PJ[b % 2][:, :], wt[:, c, ds(h * 512 + b * P, P)], xt[:, c, 0:GT], start=(n == 0), stop=(n == 5))
                        n += 1
                ins.then_inc(S["proj"], 1)

            def grams(j):
                pe.wait_ge(S["kq"], at(j * 2 + 2))
                pe.wait_ge(S["conv"], at(j * 12 + 9))
                for p in range(NP):
                    for n in range(2):
                        c0 = P * p + 64 * n
                        ins = mm(gram[64 * n:64 * n + 64, p], KQ[:, 0, c0:c0 + 64], KQ[:, :, c0:c0 + 64], start=True, stop=True)
                ins.then_inc(S["gram_mm"], 1)

            def norms(j):
                pe.wait_ge(S["sq"], at(j + 1))
                pe.wait_ge(S["conv"], at(j * 12 + 12))
                for p in range(NP):
                    ins = mm(psS[:, p:p + 1], SQ[:, 0, P * p:P * p + P], ONES[:, :], start=True, stop=True)
                ins.then_inc(S["ss_mm"], 1)

            def spread_q(j):
                pe.wait_ge(S["dq_done"], at(j + 1))
                mm(PJ[1][:, 0:256], CST[:, C_ON:C_ON + 128], DQ[:, :, :].rearrange("p a t -> p (a t)"), start=True, stop=True).then_inc(S["r_mm"], 1)

            def w_level(j, k, c):
                if k == 0:
                    pe.wait_ge(S["a_done"], at(j + 1))
                    pe.wait_ge(S["o_sub"], at(j * 2))
                else:
                    pe.wait_ge(S["z_done"], at(j * 10 + 2 * (k - 1) + c + 1))
                if k == 2:
                    pe.wait_ge(S["v_done"], at(j * 2 + 2))
                pe.nop(nofuse=True)
                for a in (2 * c, 2 * c + 1):
                    ins = per_batch(psW[c][:, a % 2], A[:, a, :], identc if k == 0 else Z[:, a, :])
                ins.then_inc(S["w_mm"], 1)

            def t_level(j, k, c):
                if k == LV - 1:
                    pe.wait_ge(S["z_done"], at(j * 10 + 2 * (k - 1) + c + 1))
                    pe.nop(nofuse=True)
                for a in (2 * c, 2 * c + 1):
                    ins = nc.tensor.transpose(psX[c][0:64, a % 2], Z[:, a, :], ident)
                ins.then_inc(S["t_mm"], 1)

            def p_level(j, k, c):
                pe.wait_ge(S["w_done"], at(j * 10 + 2 * k + c + 1))
                if k == 1:
                    pe.wait_ge(S["x_first"], at(j + 1))
                else:
                    pe.wait_ge(S["x_copied"], at(j * 16 + 4 * (k - 2) + 2 * c + 2))
                pe.nop(nofuse=True)
                for a in (2 * c, 2 * c + 1):
                    ins = per_batch(psP[c][:, a % 2], X[:, a, :], W[:, a, :])
                ins.then_inc(S["p_mm"], 1)

            def f_product(j, par, c):
                pe.wait_ge(S["x_copied"], at(j * 16 + 12 + 2 * c + 2))
                pe.wait_ge(S["gq_done"], at(j + 1))
                pe.nop(nofuse=True)
                for a in (2 * c, 2 * c + 1):
                    ins = per_batch(psF[c][:, a % 2], X[:, a, :], GQ2[:, par, a, :])
                ins.then_inc(S["f_mm"], 1)

            def g_product(j, c):
                pe.wait_ge(S["f_done"], at(j * 2 + c + 1))
                pe.nop(nofuse=True)
                for a in (2 * c, 2 * c + 1):
                    ins = per_batch(psW[c][:, a % 2], A[:, a, :], Z[:, a, :])
                ins.then_inc(S["g_mm"], 1)

            def m_product(j, c):
                pe.wait_ge(S["g_done"], at(j * 2 + c + 1))
                pe.nop(nofuse=True)
                for a in (2 * c, 2 * c + 1):
                    ins = per_batch(psP[c][:, a % 2], X[:, a, :], W[:, a, :])
                ins.then_inc(S["m_mm"], 1)

            def outputs(j, last):
                pe.wait_ge(S["m_done"], at(j * 4 + 4))
                pe.wait_ge(S["gq_done"], at(j + 1 if last else j + 2))
                pe.wait_ge(S["t1_done"], at(j + 1 if last else j + 2))
                for n, dst in enumerate(PJ):
                    for p in range(NP):
                        ins = mm(dst[:, P * p:P * p + P], V[:, p, P * n:P * n + P], M[:, p, :], start=True, stop=True)
                    ins.then_inc(S["o_mm"], 1)

            def v_transposes(i, n):
                for dst in ((BA, BB)[n],):
                    pe.wait_ge(S["conv"], at(i * 12 + 9 + 3 * n))
                    pe.wait_ge(S["f_kept"], at(i * 2))
                    for p in range(NP):
                        ins = nc.tensor.transpose(dst[:, P * p:P * p + P], Y[:, 2 + n, P * p:P * p + P], ident)
                    ins.then_inc(S["vt_mm"], 1)

            def project_out(j, h, part, last):
                p, n = part // 2, part % 2
                if part == 0:
                    pe.wait_ge(S["ot_done"], at(j * 2 + 2))
                ins = mm(AC[p // 2][:, E * (p % 2):E * (p % 2) + E], OT[:, n, P * p:P * p + P],
                         WO[:, ds(h * 2 + n, 1), :].rearrange("p o e -> p (o e)"), start=False, stop=(last and n == 1), skip_group_check=True)
                if part == 2 * NP - 1:
                    ins.then_inc(S["op_mm"], 1)
                elif last and part == NP - 1:
                    ins.then_inc(S["op_half"], 1)

            def gates(g):
                for p in range(NP):
                    for n in range(2):
                        k = 0
                        for c in range(2):
                            for xt, wt in ((XH, ABH), (XL, ABH), (XH, ABL)):
                                o = P * p + 1 - n
                                ins = mm(BB[:, 32 * p + 16 * n:32 * p + 16 * n + 16], xt[:, c, o:o + P], wt[:, c, 16 * n:16 * n + 16],
                                         start=(k == 0), stop=(k == 5))
                                k += 1
                ins.then_inc(S["gate_mm"], 1)

            def decays(g, p):
                pe.wait_ge(S["rha_done"], at(g * NP + p + 1))
                if p:
                    pe.wait_ge(S["dec_exp"], at(g * 16 + 4 * p - 2))
                for n, dst in enumerate((CA, CB)):
                    mm(dst[:, :], CST[:, C_UT:C_UT + 128], RHA[:, 8 * n:8 * n + 8, :].rearrange("p a t -> p (a t)"),
                       start=True, stop=True).then_inc(S["dec_mm"], 1)
                pe.wait_ge(S["rhq_done"], at(g * NP + p + 1))
                if p:
                    pe.wait_ge(S["dec_exp"], at(g * 16 + 4 * p))
                for n, dst in enumerate((BA, BB)):
                    mm(dst[:, :], CST[:, C_LE:C_LE + 128], RHQ[:, 8 * n:8 * n + 8, :].rearrange("p a t -> p (a t)"),
                       start=True, stop=True).then_inc(S["dec_mm"], 1)

            transposes(0)
            pe.wait_ge(S["xl_done"], at(2))
            gates(0)
            with pe.Fori(0, G) as g:
                it0 = g * NH
                project(it0, 0, 0, it0 * 2)
                project(it0, 0, 1, it0 * 2)
                pe.wait_ge(S["x3_done"], at(g * 2))
                for n in range(2):
                    mm(AC[n][:, :], ZW[:, :], XH[:, 0, 0:GT], start=True, stop=False, skip_group_check=True)
                decays(g, 0)
                decays(g, 1)
                project(it0, 0, 2)
                decays(g, 2)
                project(it0, 0, 3)
                decays(g, 3)
                grams(it0)
                norms(it0)
                pe.wait_ge(S["dec_exp"], at(g * 16 + 16))
                v_transposes(it0, 0)
                v_transposes(it0, 1)
                spread_q(it0)

                def head(j, hj, par, i, hi, first=False):
                    def earlier(*parts):
                        if not first:
                            for part in parts:
                                project_out(j - 1, hj - 1, part, False)

                    drained = j * 2 if first else j * 2 - 1
                    if i is not None:
                        project(i, hi, 0, drained, not first)
                    for k in range(1, LV - 1):
                        for c in range(2):
                            w_level(j, k, c)
                            if k > 1:
                                t_level(j, k, c)
                        if i is not None:
                            if k <= 3:
                                project(i, hi, k, drained, not first)
                            else:
                                grams(i)
                        for c in range(2):
                            p_level(j, k, c)
                        if k <= 3:
                            earlier(k - 1)
                        elif i is not None:
                            norms(i)
                    for c in range(2):
                        t_level(j, LV - 1, c)
                    earlier(3, 4)
                    for c in range(2):
                        f_product(j, par, c)
                    earlier(5)
                    for c in range(2):
                        g_product(j, c)
                    earlier(6)
                    for c in range(2):
                        m_product(j, c)
                    if i is not None:
                        spread_q(i)
                    earlier(7)
                    if i is None:
                        pe.wait_ge(S["ld_ctx"], at(g * 48 + 48))
                        pe.wait_ge(S["o_sub"], at(j * 2 + 2))
                        for c, dst in enumerate((CA, CB)):
                            mm(dst[:, :], CST[0:64, C_REP + 128 * c:C_REP + 128 * c + 128], CT[:, :], start=True, stop=True).then_inc(S["rep_mm"], 1)
                    else:
                        for c in range(2):
                            w_level(i, 0, c)
                        v_transposes(i, 0)
                    outputs(j, i is None)
                    if i is not None:
                        v_transposes(i, 1)

                for c in range(2):
                    w_level(it0, 0, c)
                head(it0, 0, 0, it0 + 1, 1, first=True)
                with pe.Fori(0, NH // 2 - 1) as h2:
                    for odd in range(2):
                        h = h2 * 2 + 1 + odd
                        head(g * NH + h, h, 1 - odd, g * NH + h + 1, h + 1)
                head(g * NH + NH - 1, NH - 1, 1, None, None)
                for part in range(2 * NP):
                    project_out(g * NH + NH - 1, NH - 1, part, True)

                transposes(g * 3 + 1)
                pe.wait_ge(S["xh_done"], at(g * 6 + 4))
                pe.wait_ge(S["kg_done"], at(g * 2 + 2))
                pe.wait_ge(S["vb_done"], at(g * 2 + 2))

                def scores(p):
                    pid = g * NP + p
                    if p:
                        pe.wait_ge(S["sub_done"], at(pid * 4))
                    for c in range(2):
                        for n in range(2):
                            b = 2 * p + n
                            for r, dst in enumerate((CA, CB, BA, BB)):
                                ins = mm(dst[64 * n:64 * n + 64, 256 * c:256 * c + 256], QT[32 * r:32 * r + 32, c, T * b:T * b + T],
                                         KG[32 * r:32 * r + 32, c, b].rearrange("p g t -> p (g t)"), start=True, stop=True, tile_position=(32 * r, 64 * n))
                    ins.then_inc(S["sc_mm"], 1)

                scores(0)
                for p in range(NP):
                    pid = g * NP + p
                    for r in range(4):
                        pe.wait_ge(S["exp_done"], at(pid * 4 + r + 1))
                        if r >= 2:
                            pe.wait_ge(S["pt_done"], at(pid * 4 + r - 1))
                        else:
                            pe.wait_ge(S["pt_done"], at(pid * 4))
                        for q in range(4):
                            ins = nc.tensor.transpose(PJ[r % 2][:, P * q:P * q + P], ES[:, q // 2, r, 2 * (q % 2):2 * (q % 2) + 2, :], ident)
                        ins.then_inc(S["pt_mm"], 1)
                    if p + 1 < NP:
                        scores(p + 1)
                    pe.wait_ge(S["pt_done"], at(pid * 4 + 4))
                    if p >= 2:
                        pe.wait_ge(S["nrm_done"], at(pid - 1))
                    for r in range(4):
                        for q in range(4):
                            kv = 4 * (q // 2) + r
                            for n in range(2):
                                b = 2 * p + n
                                col = (2 * kv + q % 2) * 18
                                ins = mm(AC[p % 2][64 * n:64 * n + 64, col:col + 18], PT[:, r, q, 64 * n:64 * n + 64],
                                         VB[:, 8 * b + kv].rearrange("p g d -> p (g d)"), start=True, stop=True)
                    ins.then_inc(S["pv_mm"], 1)

                transposes(g * 3 + 2)
                pe.wait_ge(S["xl_done"], at(g * 4 + 4))
                for f in range(FB):
                    if f >= 4:
                        pe.wait_ge(S["gelu_done"], at(g * FB + f - 3))
                    k = 0
                    for c in range(2):
                        for xt in (XH, XL):
                            ins = mm((CA, CB, BA, BB)[f % 4][:, :], W1[:, c, P * f:P * f + P], xt[:, c, 0:GT], start=(k == 0), stop=(k == 3))
                            k += 1
                    ins.then_inc(S["f1_mm"], 1)
                for f in range(FB):
                    if f == 3:
                        transposes(g * 3 + 3)
                    if f == 6:
                        pe.wait_ge(S["xl_done"], at(g * 4 + 6))
                        pe.wait_ge(S["gelu_done"], at(g * FB + FB))
                        gates(g + 1)
                    pe.wait_ge(S["hl_done"], at(g * FB + f + 1))
                    for p in range(NP):
                        for k, ht in enumerate((HH, HL)):
                            ins = mm(AC[p // 2][:, E * (p % 2):E * (p % 2) + E], ht[:, f, P * p:P * p + P], W2[:, f, :],
                                     start=(f == 0 and k == 0 and p % 2 == 0), stop=(f == FB - 1 and k == 1), skip_group_check=True)
                ins.then_inc(S["f2_mm"], 1)


_NAMES = ["x", "ctxT", "ctxR", "wall", "wo", "wab", "cw", "w1", "b1", "w2", "b2", "cst"]


def kernel(**inp):
    import numpy as _np
    import concourse.bacc as _bacc
    from concourse import mybir as _mybir
    from concourse.bass_utils import run_bass_kernel_spmd as _run

    a = {k: _np.asarray(v) for k, v in inp.items()}
    x = a["x"].reshape(G, NP, P, E).transpose(0, 2, 1, 3)
    c = a["ctx_512"]
    ctxT = c.reshape(G, 8 * T, CD).transpose(0, 2, 1)
    ctxR = c.reshape(G, 8, T, CD).transpose(0, 2, 1, 3)
    wq = a["L0_attn_Wq"].reshape(E, NH, DK)
    wk = a["L0_attn_Wk"].reshape(E, NH, DK)
    wv = a["L0_attn_Wv"].reshape(E, NH, 2 * DK)
    wall = _np.concatenate([wq, wk, wv], axis=2).reshape(2, P, NH * 512)
    wo = a["L0_attn_Wo"].reshape(2 * NH, P, E).transpose(1, 0, 2)
    wab = _np.concatenate([a["L0_attn_Wa"], a["L0_attn_Wb"]], axis=1).reshape(2, P, 32).transpose(1, 0, 2)

    def taps(w, b, n):
        return _np.concatenate([w, b[:, None]], axis=1).reshape(NH, n, P, 5)

    cw = _np.concatenate([taps(a["L0_attn_qcw"], a["L0_attn_qcb"], 1), taps(a["L0_attn_kcw"], a["L0_attn_kcb"], 1),
                          taps(a["L0_attn_vcw"], a["L0_attn_vcb"], 2)], axis=1).transpose(2, 0, 1, 3).reshape(P, NH, 20)
    w1 = a["L0_ffn_w1"].T.reshape(2, P, F).transpose(1, 0, 2).reshape(P, 2 * F)
    w2 = a["L0_ffn_w2"].T.reshape(FB, P, E).transpose(1, 0, 2).reshape(P, FB * E)
    b1 = a["L0_ffn_b1"].reshape(FB, P).T
    b2 = _np.broadcast_to(a["L0_ffn_b2"][None, :], (P, E))
    vals = dict(x=x, ctxT=ctxT, ctxR=ctxR, wall=wall, wo=wo, wab=wab, cw=cw, w1=w1, b1=b1, w2=w2, b2=b2, cst=constants())

    nc = _bacc.Bacc("TRN2", target_bir_lowering=False, num_devices=1)
    arrays, args = {}, []
    for name in _NAMES:
        v = _np.ascontiguousarray(vals[name])
        arrays[f"in_{name}"] = v
        args.append(nc.dram_tensor(f"in_{name}", v.shape, _mybir.dt.from_np(v.dtype), kind="ExternalInput").ap())
    out = nc.dram_tensor("out", (G, P, NP, E), _mybir.dt.float32, kind="ExternalOutput").ap()
    build(nc, *args, out)
    r = _run(nc, [arrays], core_ids=[0])
    y = r.results[0]["out"]
    return y.transpose(0, 2, 1, 3).reshape(NB, T, E)
```
